# Optimizing a Trainium2 kernel written in Bass

```python
import numpy as np
import jax
import jax.numpy as jnp

def _softmax(x, axis=-1):
    return jax.nn.softmax(x, axis=axis)

def _gelu(x):
    return jax.nn.gelu(x, approximate=True)

def _silu(x):
    return jax.nn.silu(x)

def _sigmoid(x):
    return jax.nn.sigmoid(x)

def _layernorm(x, axis=-1, eps=1e-05):
    m = jnp.mean(x, axis=axis, keepdims=True)
    v = jnp.var(x, axis=axis, keepdims=True)
    return (x - m) / jnp.sqrt(v + eps)

def _scatter_add(tgt, idx, src, axis=0):
    return tgt.at[idx].add(src)

def _segment_sum(src, seg, n):
    return jax.ops.segment_sum(src, seg, n)
kernel_name = 'mk_xattn_ffn_d1_seqx_r4_2b3bef'

def setup_inputs(seed: int=0):
    np.random.seed(seed)
    _w = jnp.asarray

    def _rec_inputs():
        import jax
        import jax.numpy as jnp
        _rk = jax.random.key(seed)
        x = -0.0003929 + 0.9999 * jax.random.normal(jax.random.fold_in(_rk, 1), (8, 512, 512), jnp.float32)
        _lenS = 512 - jax.random.randint(jax.random.fold_in(_rk, 7), (8,), 0, max(1, 512 // 4) + 1, jnp.int32)
        _lenS2 = 1601 - jax.random.randint(jax.random.fold_in(_rk, 8), (8,), 0, max(1, 1601 // 4) + 1, jnp.int32)
        _ctx_2048P = jax.random.normal(jax.random.fold_in(_rk, 11), (8, 16, 512), jnp.float32)
        _ctx_2048c = jax.random.dirichlet(jax.random.fold_in(_rk, 511), 0.3 * jnp.ones((16,), jnp.float32), (8, 1601))
        _ctx_2048t = jnp.einsum('bsk,bkd->bsd', _ctx_2048c, _ctx_2048P)
        _ctx_2048t = _ctx_2048t * jax.lax.rsqrt(jnp.mean(jnp.square(_ctx_2048t)) + 1e-12) * 0.953939
        ctx_2048 = -0.000514642 + 1.00011 * (_ctx_2048t + 0.3 * jax.random.normal(jax.random.fold_in(_rk, 611), (8, 1601, 512), jnp.float32))
        return (x, ctx_2048)
    x, ctx_2048 = _rec_inputs()

    def _L0_xattn_setup():
        import jax, jax.numpy as jnp
        import numpy as np
        NUM_HEADS = 16

        def _qdq(x):
            s = jnp.maximum(jnp.max(jnp.abs(x), axis=-1, keepdims=True) / 127.0, 1e-08)
            return jnp.clip(jnp.round(x / s), -127.0, 127.0) * s
        key = jax.random.key(seed)
        ks = jax.random.split(key, 8)
        B, N, M, D = (2, 1024, 128, 512)
        w_std = 0.02
        return {'x': jax.random.normal(ks[0], (B, N, D), jnp.float32), 'cond': jax.random.normal(ks[1], (B, M, D), jnp.float32), 'wq': jax.random.normal(ks[2], (D, D), jnp.float32) * w_std, 'bq': jax.random.normal(ks[3], (D,), jnp.float32) * w_std, 'wkv': jax.random.normal(ks[4], (2 * D, D), jnp.float32) * w_std, 'bkv': jax.random.normal(ks[5], (2 * D,), jnp.float32) * w_std, 'wp': jax.random.normal(ks[6], (D, D), jnp.float32) * w_std, 'bp': jax.random.normal(ks[7], (D,), jnp.float32) * w_std}
    _L0_xattn_all = _L0_xattn_setup()
    _L0_xattn_in = {k: v for k, v in _L0_xattn_all.items() if k in ('wq', 'bq', 'wkv', 'bkv', 'wp', 'bp')}
    del _L0_xattn_all

    def _L0_ffn_setup():
        import jax, jax.numpy as jnp
        import numpy as np
        B, S, D = (4, 512, 512)
        E, K, M = (8, 2, 256)
        key = jax.random.key(seed)
        k0, k1, k2, k3, k4 = jax.random.split(key, 5)
        d_scale = D ** (-0.5)
        m_scale = M ** (-0.5)
        return {'x': jax.random.normal(k0, (B, S, D), jnp.float32), 'w_gate': jax.random.normal(k1, (D, E), jnp.float32) * d_scale, 'wi_0': jax.random.normal(k2, (E, D, M), jnp.float32) * d_scale, 'wi_1': jax.random.normal(k3, (E, D, M), jnp.float32) * d_scale, 'wo': jax.random.normal(k4, (E, M, D), jnp.float32) * m_scale}
    _L0_ffn_all = _L0_ffn_setup()
    _L0_ffn_in = {k: v for k, v in _L0_ffn_all.items() if k in ('w_gate', 'wi_0', 'wi_1', 'wo')}
    del _L0_ffn_all
    return {'x': x, 'ctx_2048': ctx_2048, 'L0_xattn_wq': _L0_xattn_in['wq'], 'L0_xattn_bq': _L0_xattn_in['bq'], 'L0_xattn_wkv': _L0_xattn_in['wkv'], 'L0_xattn_bkv': _L0_xattn_in['bkv'], 'L0_xattn_wp': _L0_xattn_in['wp'], 'L0_xattn_bp': _L0_xattn_in['bp'], 'L0_ffn_w_gate': _L0_ffn_in['w_gate'], 'L0_ffn_wi_0': _L0_ffn_in['wi_0'], 'L0_ffn_wi_1': _L0_ffn_in['wi_1'], 'L0_ffn_wo': _L0_ffn_in['wo']}

def reference(x, ctx_2048, L0_xattn_wq, L0_xattn_bq, L0_xattn_wkv, L0_xattn_bkv, L0_xattn_wp, L0_xattn_bp, L0_ffn_w_gate, L0_ffn_wi_0, L0_ffn_wi_1, L0_ffn_wo):
    import jax
    import jax.numpy as jnp

    def _L0_xattn_ref(x, cond, wq, bq, wkv, bkv, wp, bp):
        import jax, jax.numpy as jnp
        import numpy as np
        NUM_HEADS = 16

        def _qdq(x):
            s = jnp.maximum(jnp.max(jnp.abs(x), axis=-1, keepdims=True) / 127.0, 1e-08)
            return jnp.clip(jnp.round(x / s), -127.0, 127.0) * s
        B, N, C = x.shape
        M = cond.shape[1]
        H = NUM_HEADS
        Dh = C // H
        q = _qdq(x) @ _qdq(wq).T + bq
        kv = cond @ wkv.T + bkv
        k, v = jnp.split(kv, 2, axis=-1)
        q = q.reshape(B, N, H, Dh)
        k = k.reshape(B, M, H, Dh)
        v = v.reshape(B, M, H, Dh)
        scale = 1.0 / np.sqrt(Dh)
        attn = jax.nn.softmax(jnp.einsum('bnhd,bmhd->bhnm', q, k) * scale, axis=-1)
        o = jnp.einsum('bhnm,bmhd->bnhd', attn, v).reshape(B, N, C)
        out = _qdq(o) @ _qdq(wp).T + bp
        return out

    def _L0_ffn_ref(x, w_gate, wi_0, wi_1, wo):
        import jax, jax.numpy as jnp
        import numpy as np
        B, S, D = (4, 512, 512)
        E, K, M = (8, 2, 256)
        b, s, d = x.shape
        e = w_gate.shape[1]
        xf = x.reshape(-1, d)
        logits = jnp.dot(xf, w_gate)
        top_logits, top_idx = jax.lax.top_k(logits, K)
        weights = jax.nn.softmax(top_logits, axis=-1)
        flat_idx = top_idx.reshape(-1)
        sort_order = jnp.argsort(flat_idx)
        token_ids = sort_order // K
        sorted_x = jnp.take(xf, token_ids, axis=0)
        group_sizes = jnp.bincount(flat_idx, length=E).astype(jnp.int32)
        h0 = jax.lax.ragged_dot(sorted_x, wi_0, group_sizes)
        h1 = jax.lax.ragged_dot(sorted_x, wi_1, group_sizes)
        inter = jax.nn.silu(h0) * h1
        out_sorted = jax.lax.ragged_dot(inter, wo, group_sizes)
        unsort = jnp.argsort(sort_order)
        out = jnp.take(out_sorted, unsort, axis=0).reshape(-1, K, d)
        out = jnp.einsum('tkd,tk->td', out, weights)
        return out.reshape(b, s, d)
    x = x + _L0_xattn_ref(_layernorm(x, axis=-1), ctx_2048, L0_xattn_wq, L0_xattn_bq, L0_xattn_wkv, L0_xattn_bkv, L0_xattn_wp, L0_xattn_bp)
    x = x + _L0_ffn_ref(_layernorm(x, axis=-1), L0_ffn_w_gate, L0_ffn_wi_0, L0_ffn_wi_1, L0_ffn_wo)
    return x

_drawn_inputs = setup_inputs


def setup_inputs(seed=0):
    import zlib

    import numpy as np

    out = dict(_drawn_inputs(seed))
    spreads = {}
    factors = {'L0_xattn_bq': 38.053}
    for name, (base, spread) in spreads.items():
        noise = np.random.default_rng([zlib.crc32(name.encode()), seed]).standard_normal(out[name].shape)
        drawn = base * np.exp(spread * noise) if base else spread * noise
        out[name] = jnp.asarray(drawn.astype(out[name].dtype))
    for name, factor in factors.items():
        out[name] = (out[name] * factor).astype(out[name].dtype)
    return out
```

```python
from contextlib import ExitStack, contextmanager

import concourse.bass as bass
from concourse import mybir

F32 = mybir.dt.float32
F16 = mybir.dt.float16
BF16 = mybir.dt.bfloat16
I32 = mybir.dt.int32
U32 = mybir.dt.uint32
ALU = mybir.AluOpType
ACT = mybir.ActivationFunctionType
AX = mybir.AxisListType

P = 128
B, N, C = 8, 512, 512
M = 1601
H, DH = 16, 32
E, TOPK, FF = 8, 2, 256
CC = C // P
QT = N // P
HB = P // DH
NBLK = H // HB
KT = -(-M // P)
TAIL = M - (KT - 1) * P
VC = 2 * DH + 1
WSCALE = 64.0
EPS = 1e-5
ROUND = 12582912.0
QMAX = 127.0


@contextmanager
def phase(nc):
    with ExitStack() as held:
        sems = []

        def sem(name):
            sems.append(held.enter_context(nc.semaphore(name)))
            return sems[-1]

        with nc.Block() as block:
            yield block, sem
        for s in sems:
            nc.gpsimd.sem_clear(s)
        nc.all_engine_barrier()


class Steps:

    def __init__(self, eng, sem):
        self.eng, self.sem, self.n = eng, sem, 0

    def __call__(self, ins):
        self.n += 1
        ins.then_inc(self.sem, 1)
        self.eng.wait_ge(self.sem, self.n)


def sbuf(nc, held, name, shape, dt):
    return held.enter_context(nc.sbuf_tensor(name, shape, dt))


def banks(nc, held, names, dt=F32):
    n = 512 if dt == F32 else 1024
    return [held.enter_context(nc.psum_tensor(x, [P, n], dt)) for x in names]


def make_constants(nc, held):
    k = {
        "id32": sbuf(nc, held, "id32", [P, P], F32),
        "id16": sbuf(nc, held, "id16", [P, P], F16),
        "idb": sbuf(nc, held, "idb", [P, P], BF16),
        "ones": sbuf(nc, held, "ones", [P, P], F32),
    }
    with phase(nc) as (block, sem):
        filled, cut = sem("filled"), sem("cut")

        @block.gpsimd
        def _(pool):
            pool.memset(k["ones"][:, :], 1.0).then_inc(filled, 1)
            pool.wait_ge(filled, 1)
            pool.affine_select(out=k["id32"][:, :], in_=k["ones"][:, :], compare_op=ALU.is_equal, fill=0.0,
                               base=0, pattern=[[-1, P]], channel_multiplier=1).then_inc(cut, 1)

        @block.vector
        def _(dve):
            dve.wait_ge(cut, 1)
            dve.tensor_copy(k["id16"][:, :], k["id32"][:, :])
            dve.tensor_copy(k["idb"][:, :], k["id32"][:, :])
    return k


def quantize_weight(nc, k, tag, w, w_t, s_row):
    with ExitStack() as held, phase(nc) as (block, sem):
        w_n = sbuf(nc, held, tag + "w_n", [P, CC, C], F32)
        w_y = sbuf(nc, held, tag + "w_y", [P, CC, C], F32)
        w_q = sbuf(nc, held, tag + "w_q", [P, CC, C], BF16)
        amax = sbuf(nc, held, tag + "w_amax", [P, CC], F32)
        scale = sbuf(nc, held, tag + "w_scale", [P, CC], F32)
        inv = sbuf(nc, held, tag + "w_inv", [P, CC], F32)
        diag = sbuf(nc, held, tag + "w_diag", [P, CC, P], F32)
        ps_t = banks(nc, held, [tag + "ps_t0", tag + "ps_t1"], BF16)
        ps_s = banks(nc, held, [tag + "ps_s"])[0]
        loaded, step, quantized, spread, turned, rowed = (
            sem(x) for x in ("w_loaded", "w_step", "w_quantized", "w_spread", "w_turned", "w_rowed"))

        @block.sync
        def _(sp):
            sp.dma_start(w_n[:, :, :], w.rearrange("(t p) c -> p t c", p=P)).then_inc(loaded, 16)

        @block.vector
        def _(dve):
            done = Steps(dve, step)
            dve.wait_ge(loaded, 16)
            done(dve.tensor_reduce(amax[:, :], w_n[:, :, :], AX.X, ALU.max, apply_absolute_value=True))
            done(dve.tensor_scalar(scale[:, :], amax[:, :], 1.0 / QMAX, 1e-8, ALU.mult, ALU.max))
            done(dve.reciprocal(inv[:, :], scale[:, :]))
            for t in range(CC):
                dve.tensor_scalar(w_y[:, t, :], w_n[:, t, :], inv[:, t:t + 1], QMAX, ALU.mult, ALU.min)
                last = dve.tensor_scalar(diag[:, t, :], k["id32"][:, :], scale[:, t:t + 1], None, ALU.mult)
            last.then_inc(spread, 1)
            dve.wait_ge(spread, 1)
            done(dve.tensor_scalar(w_n[:, :, :], w_y[:, :, :], -QMAX, ROUND, ALU.max, ALU.add))
            dve.tensor_scalar(w_q[:, :, :], w_n[:, :, :], ROUND, None, ALU.subtract).then_inc(quantized, 1)
            for half in range(2):
                dve.wait_ge(turned, half + 1)
                dve.tensor_copy(w_t[:, 2 * half:2 * half + 2, :],
                                ps_t[half][:, :].rearrange("p (c o) -> p c o", c=2))
            dve.wait_ge(rowed, 1)
            dve.tensor_copy(s_row[:, :], ps_s[:, :])

        @block.tensor
        def _(pe):
            pe.wait_ge(spread, 1)
            for t in range(CC):
                last = pe.matmul(ps_s[:, t * P:(t + 1) * P], k["ones"][:, :], diag[:, t, :], start=True, stop=True)
            last.then_inc(rowed, 1)
            pe.wait_ge(quantized, 1)
            for half in range(2):
                for c in range(2 * half, 2 * half + 2):
                    for t in range(CC):
                        at = (c % 2) * C + t * P
                        last = pe.transpose(ps_t[half][:, at:at + P], w_q[:, t, c * P:(c + 1) * P], k["idb"][:, :])
                last.then_inc(turned, 1)


def split_kv_weight(nc, wkv_t, wkv):
    with ExitStack() as held, phase(nc) as (block, sem):
        raw = sbuf(nc, held, "kv_raw", [P, CC, 2 * C], F32)
        loaded, high = sem("kv_loaded"), sem("kv_high")

        @block.sync
        def _(sp):
            for c in range(CC):
                sp.dma_start(raw[:, c, :], wkv_t[c * P:(c + 1) * P, :]).then_inc(loaded, 16)

        @block.vector
        def _(dve):
            dve.wait_ge(loaded, 16 * CC)
            for c in range(CC):
                dve.tensor_scalar(wkv[:, 0, c, :], raw[:, c, :], WSCALE, None, ALU.mult).then_inc(high, 1)
            for c in range(CC):
                dve.wait_ge(high, c + 1)
                dve.scalar_tensor_tensor(out=wkv[:, 1, c, :], in0=raw[:, c, :], scalar=WSCALE,
                                         in1=wkv[:, 0, c, :], op0=ALU.mult, op1=ALU.subtract)


def inverse_std(dve, done, var, std, rstd, tmp):
    done(dve.reciprocal(rstd, std))
    done(dve.tensor_tensor(tmp, rstd, rstd, ALU.mult))
    done(dve.scalar_tensor_tensor(out=tmp, in0=var, scalar=EPS, in1=tmp, op0=ALU.add, op1=ALU.mult))
    done(dve.tensor_scalar(tmp, tmp, -0.5, 1.5, ALU.mult, ALU.add))
    done(dve.tensor_tensor(rstd, rstd, tmp, ALU.mult))


def project_queries(nc, k, x, wq_t, s_row, bq_row, q_nat, q_t):
    with ExitStack() as held:
        xt = sbuf(nc, held, "xt", [P, QT, C], F32)
        xm = sbuf(nc, held, "xm", [P, QT, C], F32)
        xy = sbuf(nc, held, "xy", [P, QT, C], F32)
        xq = sbuf(nc, held, "xq", [P, QT, C], BF16)
        xqt = sbuf(nc, held, "xqt", [P, CC, N], BF16)
        q = sbuf(nc, held, "q", [P, QT, C], F32)
        q_hl = sbuf(nc, held, "q_hl", [P, 2, QT, C], F16)
        q_tt = sbuf(nc, held, "q_tt", [P, 2, NBLK, N], F16)
        st = sbuf(nc, held, "st", [P, QT, 6], F32)
        mv = sbuf(nc, held, "mv", [P, QT, 2], F32)
        nmean = sbuf(nc, held, "nmean", [P, QT], F32)
        std, rstd, tmp, amax, sx, inv, mul = (
            sbuf(nc, held, "q_" + x, [P, QT], F32) for x in ("std", "rstd", "tmp", "amax", "sx", "inv", "mul"))
        ps_q = banks(nc, held, [f"q_ps{t}" for t in range(QT)])
        ps_x = banks(nc, held, ["q_px0", "q_px1"], BF16)
        ps_t = banks(nc, held, ["q_pt0", "q_pt1"], F16)
        with nc.Fori(0, B) as b, phase(nc) as (block, sem):
            loaded, step, centred, rooted, rows, quantized, turned, xqt_ready, projected = (
                sem("q_" + x) for x in ("loaded", "step", "centred", "rooted", "rows", "quantized", "turned",
                                        "xqt_ready", "projected"))
            q_ready, high, split, q_turned, tt_ready, stored = (
                sem("q_" + x) for x in ("ready", "high", "split", "qturned", "tt_ready", "stored"))

            @block.sync
            def _(sp):
                sp.dma_start(xt[:, :, :], x[bass.ds(b * N, N), :].rearrange("(t p) c -> p t c", p=P)).then_inc(loaded, 16)
                sp.wait_ge(q_ready, 1)
                sp.dma_start(q_nat[bass.ds(b * N, N), :].rearrange("(t p) c -> p t c", p=P), q[:, :, :]).then_inc(stored, 16)
                for part in range(2):
                    sp.wait_ge(tt_ready, 2 * part + 2)
                    sp.dma_start(q_t[part, :, :, bass.ds(b * N, N)].rearrange("k p n -> p k n"),
                                 q_tt[:, part, :, :]).then_inc(stored, 16)
                sp.wait_ge(stored, 48)

            @block.scalar
            def _(act):
                act.wait_ge(centred, 1)
                act.activation(std[:, :], mv[:, :, 1], ACT.Sqrt, bias=k["eps"][:, 0:1]).then_inc(rooted, 1)
                for t in range(QT):
                    last = act.activation(xm[:, t, :], xt[:, t, :], ACT.Identity, bias=nmean[:, t:t + 1])
                last.then_inc(rooted, 1)
                for half in range(2):
                    act.wait_ge(turned, half + 1)
                    act.copy(xqt[:, 2 * half:2 * half + 2, :],
                             ps_x[half][:, :].rearrange("p (c n) -> p c n", c=2)).then_inc(xqt_ready, 1)
                act.wait_ge(q_ready, 1)
                act.copy(q_hl[:, 0, :, :], q[:, :, :]).then_inc(high, 1)
                for g in range(4):
                    act.wait_ge(q_turned, g + 1)
                    act.copy(q_tt[:, g // 2, 2 * (g % 2):2 * (g % 2) + 2, :],
                             ps_t[g % 2][:, :].rearrange("p (c n) -> p c n", c=2)).then_inc(tt_ready, 1)

            @block.vector
            def _(dve):
                done = Steps(dve, step)
                dve.wait_ge(loaded, 16)
                for t in range(QT):
                    last = dve.bn_stats(st[:, t, :], xt[:, t, :])
                done(last)
                for t in range(QT):
                    last = dve.bn_aggr(mv[:, t, :], st[:, t, :])
                done(last)
                dve.tensor_scalar(nmean[:, :], mv[:, :, 0], -1.0, None, ALU.mult).then_inc(centred, 1)
                dve.wait_ge(rooted, 1)
                inverse_std(dve, done, mv[:, :, 1], std[:, :], rstd[:, :], tmp[:, :])
                dve.wait_ge(rooted, 2)
                done(dve.tensor_reduce(amax[:, :], xm[:, :, :], AX.X, ALU.max, apply_absolute_value=True))
                done(dve.tensor_tensor(sx[:, :], amax[:, :], rstd[:, :], ALU.mult))
                done(dve.tensor_scalar(sx[:, :], sx[:, :], 1.0 / QMAX, 1e-8, ALU.mult, ALU.max))
                done(dve.reciprocal(inv[:, :], sx[:, :]))
                done(dve.tensor_tensor(mul[:, :], inv[:, :], rstd[:, :], ALU.mult))
                for t in range(QT):
                    last = dve.tensor_scalar(xy[:, t, :], xm[:, t, :], mul[:, t:t + 1], QMAX, ALU.mult, ALU.min)
                done(last)
                done(dve.tensor_scalar(xm[:, :, :], xy[:, :, :], -QMAX, ROUND, ALU.max, ALU.add))
                dve.tensor_scalar(xq[:, :, :], xm[:, :, :], ROUND, None, ALU.subtract).then_inc(quantized, 1)
                for t in range(QT):
                    dve.wait_ge(projected, t + 1)
                    last = dve.scalar_tensor_tensor(out=q[:, t, :], in0=ps_q[t][:, :], scalar=sx[:, t:t + 1],
                                                    in1=s_row[:, :], op0=ALU.mult, op1=ALU.mult)
                done(last)
                dve.tensor_tensor(q[:, :, :], q[:, :, :], bq_row[:, None, :].to_broadcast([P, QT, C]),
                                  ALU.add).then_inc(q_ready, 1)
                dve.wait_ge(high, 1)
                dve.tensor_tensor(q_hl[:, 1, :, :], q[:, :, :], q_hl[:, 0, :, :], ALU.subtract).then_inc(split, 1)

            @block.tensor
            def _(pe):
                pe.wait_ge(quantized, 1)
                for half in range(2):
                    for c in range(2 * half, 2 * half + 2):
                        for t in range(QT):
                            at = (c % 2) * N + t * P
                            last = pe.transpose(ps_x[half][:, at:at + P], xq[:, t, c * P:(c + 1) * P], k["idb"][:, :])
                    last.then_inc(turned, 1)
                pe.wait_ge(xqt_ready, 2)
                for t in range(QT):
                    for c in range(CC):
                        last = pe.matmul(ps_q[t][:, :], xqt[:, c, t * P:(t + 1) * P], wq_t[:, c, :],
                                         start=(c == 0), stop=(c == CC - 1))
                    last.then_inc(projected, 1)
                for g in range(4):
                    if g == 0:
                        pe.wait_ge(high, 1)
                    if g == 2:
                        pe.wait_ge(split, 1)
                    if g >= 2:
                        pe.wait_ge(tt_ready, g - 1)
                    for kb in range(2 * (g % 2), 2 * (g % 2) + 2):
                        for t in range(QT):
                            at = (kb % 2) * N + t * P
                            last = pe.transpose(ps_t[g % 2][:, at:at + P], q_hl[:, g // 2, t, kb * P:(kb + 1) * P],
                                                k["id16"][:, :])
                    last.then_inc(q_turned, 1)


TERMS = 3
GROUP = 2
GROUPS = -(-KT // GROUP)
SLOTS = HB * GROUPS
LAG = 3
NP = 4
KEY_CUTS = [0, 401, 801, 1201, M]
VALUE_TILES = [range(0, 4), range(4, 7), range(7, 10), range(10, KT)]
HALVES = [(0, 801), (801, M)]
SUM_LOW, SUM_HIGH = 0.5, float(2 ** 20)
OUT_HIGH = 1e30


def group_tiles(g):
    return range(GROUP * g, min(GROUP * g + GROUP, KT))


def rows_of(kt):
    return P if kt < KT - 1 else TAIL


class Jobs:

    def __init__(self, units, attend, last):
        self.all = []
        self.slices = {}
        self.ends = {}
        self.keys_done = {}
        self.context_done = {}
        for v in units:
            new = [("k", v + 1, g) for g in range(4)] if v + 1 < 2 * NBLK or not last else []
            if v < 0:
                new += [("v", 0, t) for t in range(KT)]
            elif v < NBLK or not last:
                new += [("v", (v // NBLK + 1) % 2, t) for t in VALUE_TILES[v % NBLK]]
            at = max(v, 0) * SLOTS
            for n, job in enumerate(new):
                j = len(self.all)
                self.all.append(job)
                for part in range(TERMS):
                    s = at + (n * TERMS + part if attend else n)
                    self.slices.setdefault(s, []).append((j, part))
                self.ends.setdefault(s, []).append(j)
                if job[0] == "k":
                    self.keys_done[v + 1] = j + 1
            self.context_done[v] = len(self.all)
        self.slots = (max(units) + 1) * SLOTS if attend else len(self.all)


def attention_pass(nc, t, i, units, attend, last, loads):
    jobs = Jobs(units, attend, last)
    ends_by = {}
    with phase(nc) as (block, sem):
        scores, shifted, lows, used = (sem("a_" + x) for x in ("scores", "exp", "lows", "used"))
        projected, highs, job_done = (sem("a_" + x) for x in ("projected", "highs", "job_done"))
        keys_in, queries_in, ctx_in, out_stored = (
            [sem(f"a_{x}{n}") for n in range(2)] for x in ("keys_in", "queries_in", "ctx_in", "out_stored"))
        ctx_high, ctx_split = sem("a_ctx_high"), sem("a_ctx_split")
        out_copied, inverted, out_step, out_ready, checked, check_step = (
            sem("a_" + x) for x in ("out_copied", "inverted", "out_step", "out_ready", "checked", "check_step"))
        stacked = sorted(jobs.keys_done)

        def loads_of(v):
            return sum(1 for u in stacked if u % 2 == v % 2 and u <= v)

        piece = [(n, c, h) for n in range(len(loads)) for c in range(CC) for h in range(2)]

        def batch_of(v):
            return 2 * i + v // NBLK if v >= 0 else 0

        def slot_pieces(s):
            out = []
            for p, (n, c, h) in enumerate(piece):
                at = loads[n][0] * SLOTS + 3 * (c * 2 + h) if attend else 0
                if at == s:
                    out.append(p)
            return out

        @block.sync
        def _(sp):
            def load_queries(v):
                if attend and v - 2 >= 0:
                    sp.wait_ge(scores, SLOTS * (v - 1))
                for s in range(TERMS):
                    kb = v % NBLK
                    sp.dma_start(t["q_stack"][v % 2][s * DH:(s + 1) * DH, :, :],
                                 t["q_t"][1 if s == 2 else 0, kb, :, bass.ds(batch_of(v) * N, N)]
                                 .rearrange("(j d) n -> d j n", d=DH)).then_inc(queries_in[v % 2], 16)

            def stack_keys(v):
                sp.wait_ge(job_done, jobs.keys_done[v])
                for j in range(HB):
                    for s in range(TERMS):
                        sp.dma_start(t["k_stack"][v % 2][s * DH:(s + 1) * DH, j, :],
                                     t["k_parts"][j * DH:(j + 1) * DH, s % 2, :]).then_inc(keys_in[v % 2], 16)

            def load_context(n):
                v, par, batch = loads[n]
                for c in range(CC):
                    for h, (a, b) in enumerate(HALVES):
                        p = n * 2 * CC + 2 * c + h
                        if p >= 2:
                            sp.wait_ge(ctx_split, p - 1)
                        sp.dma_start(t["ctx_raw"][p % 2][:, 0:b - a],
                                     t["ctx_t"][bass.ds(batch, 1), c * P:(c + 1) * P, a:b]
                                     .rearrange("a p n -> p (a n)")).then_inc(ctx_in[p % 2], 16)

            def store_out(v):
                sp.wait_ge(out_ready, v + 1)
                sp.dma_start(t["o"][bass.ds(batch_of(v) * N, N), (v % NBLK) * P:(v % NBLK + 1) * P]
                             .rearrange("(t p) c -> p t c", p=P), t["o_tile"][v % 2][:, :, :]).then_inc(out_stored[v % 2], 16)

            for v in units:
                if v + 1 < 2 * NBLK or not last:
                    load_queries(v + 1)
                for n in range(len(loads)):
                    if loads[n][0] == v:
                        load_context(n)
                if v + 1 in jobs.keys_done:
                    stack_keys(v + 1)
                if attend and v >= 1:
                    store_out(v - 1)
            if attend:
                store_out(units[-1])
                for n in range(2):
                    sp.wait_ge(out_stored[n], 16 * len(units) // 2)
            v = stacked[-1]
            sp.wait_ge(queries_in[v % 2], 16 * TERMS * loads_of(v))
            sp.wait_ge(keys_in[v % 2], 16 * TERMS * HB * loads_of(v))

        @block.tensor
        def _(pe):
            def do_scores(s):
                v, j, g = s // SLOTS, s % SLOTS // GROUPS, s % GROUPS
                if s >= 2:
                    pe.wait_ge(shifted, s - 1)
                if s % SLOTS == 0 and v > 0:
                    pe.wait_ge(keys_in[v % 2], 16 * TERMS * HB * loads_of(v))
                    pe.wait_ge(queries_in[v % 2], 16 * TERMS * loads_of(v))
                for n, kt in enumerate(group_tiles(g)):
                    r = rows_of(kt)
                    mm = pe.matmul(t["ps_s"][s % 2][0:r, n * N:(n + 1) * N],
                                   t["k_stack"][v % 2][0:TERMS * DH, j, kt * P:kt * P + r],
                                   t["q_stack"][v % 2][0:TERMS * DH, j, :], start=True, stop=True)
                mm.then_inc(scores, 1)

            def project(j, part):
                kind, where, n = jobs.all[j]
                if kind == "k":
                    par = where // NBLK % 2
                    c0, a, b = where % NBLK * P, KEY_CUTS[n], KEY_CUTS[n + 1]
                    rows, cols = P, b - a
                else:
                    par, rows, cols = where, rows_of(n), C
                if part == 0:
                    if j >= 2:
                        pe.wait_ge(job_done, j - 1)
                    for m, (v, p, _) in enumerate(loads):
                        if p == par and (not attend or j >= jobs.context_done[v]):
                            pe.wait_ge(ctx_split, 2 * CC * (m + 1))
                ps = t["ps_p"][j % 2][0:rows, 0:cols]
                for m in range(CC * part, CC * part + CC):
                    c, term = m // TERMS, m % TERMS
                    w_part, x_part = (0, 0, 1)[term], (0, 1, 0)[term]
                    ctx = t["ctx"][par]
                    if kind == "k":
                        lhs, rhs = t["wkv"][:, w_part, c, c0:c0 + P], ctx[:, x_part, c, a:b]
                    else:
                        lhs, rhs = ctx[:, x_part, c, n * P:n * P + rows], t["wkv"][:, w_part, c, C:2 * C]
                    mm = pe.matmul(ps, lhs, rhs, start=(m == 0), stop=(m == TERMS * CC - 1))
                if part == TERMS - 1:
                    mm.then_inc(projected, 1)

            def do_values(s):
                v, j, g = s // SLOTS, s % SLOTS // GROUPS, s % GROUPS
                head = s // GROUPS
                pe.wait_ge(lows, s + 1)
                if g == 0 and head >= 2:
                    pe.wait_ge(out_copied, head - 1)
                p_high = t["p"][s % NP][:, :].bitcast(BF16).rearrange("p (n two) -> p n two", two=2)[:, :, 1]
                for n, kt in enumerate(group_tiles(g)):
                    r = rows_of(kt)
                    val = t["v"][v // NBLK % 2][0:r, kt, (v % NBLK) * HB + j, :]
                    for low, part in enumerate((p_high, t["p_low"][s % NP])):
                        for q in range(QT):
                            mm = pe.matmul(t["ps_o"][head % 2][:, q * VC:(q + 1) * VC],
                                           part[0:r, n * N + q * P:n * N + (q + 1) * P], val,
                                           start=(g == 0 and n == 0 and low == 0 and q == 0),
                                           stop=(kt == KT - 1 and low == 1), skip_group_check=True)
                mm.then_inc(used, 1)

            for s in range(jobs.slots):
                if attend:
                    do_scores(s)
                for j, part in jobs.slices.get(s, []):
                    project(j, part)
                if attend and s >= LAG:
                    do_values(s - LAG)
            if attend:
                for s in range(jobs.slots - LAG, jobs.slots):
                    do_values(s)

        @block.scalar
        def _(act):
            def exponentials(s):
                g = s % GROUPS
                tiles = group_tiles(g)
                r = rows_of(tiles[-1])
                act.wait_ge(scores, s + 1)
                if s >= NP:
                    act.wait_ge(used, s - NP + 1)
                act.activation(t["p"][s % NP][0:r, 0:len(tiles) * N], t["ps_s"][s % 2][0:r, 0:len(tiles) * N],
                               ACT.Exp, scale=float(DH) ** -0.5 / WSCALE).then_inc(shifted, 1)

            def job_high(j):
                kind, where, n = jobs.all[j]
                act.wait_ge(projected, j + 1)
                if kind == "k":
                    a, b = KEY_CUTS[n], KEY_CUTS[n + 1]
                    if n == 0 and loads_of(where - 1):
                        act.wait_ge(keys_in[(where - 1) % 2], 16 * TERMS * HB * loads_of(where - 1))
                    act.activation(t["k_parts"][:, 0, a:b], t["ps_p"][j % 2][:, 0:b - a], ACT.Identity,
                                   bias=t["bk"][:, where % NBLK:where % NBLK + 1]).then_inc(highs, 1)
                else:
                    r = rows_of(n)
                    if attend and j in first_value and where == 0:
                        act.wait_ge(used, NBLK * SLOTS)
                    act.copy(t["v"][where][0:r, n, :, 0:DH],
                             t["ps_p"][j % 2][0:r, :].rearrange("p (h d) -> p h d", d=DH)).then_inc(highs, 1)

            def copy_out(head):
                v, j = head // HB, head % HB
                act.wait_ge(used, GROUPS * (head + 1))
                if j == 0 and v >= 2:
                    act.wait_ge(out_ready, v - 1)
                act.copy(t["o_sums"][v % 2][:, j, :, :],
                         t["ps_o"][head % 2][:, 0:QT * VC].rearrange("p (q c) -> p q c", q=QT)).then_inc(out_copied, 1)

            def context_high(p):
                n, c, h = piece[p]
                a, b = HALVES[h]
                act.wait_ge(ctx_in[p % 2], 16 * (p // 2 + 1))
                if attend and (c, h) == (0, 0):
                    act.wait_ge(job_done, jobs.context_done[loads[n][0] - 1])
                act.copy(t["ctx"][loads[n][1]][:, 0, c, a:b], t["ctx_raw"][p % 2][:, 0:b - a]).then_inc(ctx_high, 1)

            first_value = {min([j for j, x in enumerate(jobs.all) if x[0] == "v" and x[1] == 0], default=-1)}
            if not attend:
                for p in range(len(piece)):
                    context_high(p)
            for s in range(jobs.slots):
                if attend:
                    exponentials(s)
                for j in jobs.ends.get(s - 1 if attend else s, []):
                    job_high(j)
                if attend:
                    for p in slot_pieces(s):
                        context_high(p)
                    if s > LAG and (s - LAG) % GROUPS == 0:
                        copy_out((s - LAG) // GROUPS - 1)
            if attend:
                for j in jobs.ends.get(jobs.slots - 1, []):
                    job_high(j)
                copy_out(jobs.slots // GROUPS - 1)

        @block.vector
        def _(dve):
            done = Steps(dve, check_step)

            def low_probabilities(s):
                g = s % GROUPS
                tiles = group_tiles(g)
                r, n = rows_of(tiles[-1]), len(tiles) * N
                dve.wait_ge(shifted, s + 1)
                full = t["p"][s % NP][0:r, 0:n]
                high = full.bitcast(BF16).rearrange("p (n two) -> p n two", two=2)[:, :, 1]
                dve.tensor_tensor(t["p_low"][s % NP][0:r, 0:n], full, high, ALU.subtract).then_inc(lows, 1)

            def job_low(j):
                kind, where, n = jobs.all[j]
                dve.wait_ge(highs, j + 1)
                if kind == "k":
                    a, b = KEY_CUTS[n], KEY_CUTS[n + 1]
                    dve.scalar_tensor_tensor(out=t["k_parts"][:, 1, a:b], in0=t["ps_p"][j % 2][:, 0:b - a],
                                             scalar=t["bk"][:, where % NBLK:where % NBLK + 1],
                                             in1=t["k_parts"][:, 0, a:b], op0=ALU.add,
                                             op1=ALU.subtract).then_inc(job_done, 1)
                else:
                    r = rows_of(n)
                    dve.tensor_tensor(t["v"][where][0:r, n, :, DH:2 * DH],
                                      t["ps_p"][j % 2][0:r, :].rearrange("p (h d) -> p h d", d=DH),
                                      t["v"][where][0:r, n, :, 0:DH], ALU.subtract).then_inc(job_done, 1)

            def invert(v):
                dve.wait_ge(out_copied, HB * (v + 1))
                if v >= 2:
                    dve.wait_ge(out_ready, v - 1)
                sums = t["o_sums"][v % 2][:, :, :, 2 * DH]
                dve.reciprocal(t["o_inv"][v % 2][:, :, :], sums).then_inc(inverted, 1)
                done(dve.scalar_tensor_tensor(out=t["fine"][:, :, :], in0=sums, scalar=SUM_LOW * WSCALE,
                                              in1=t["fine"][:, :, :], op0=ALU.is_ge, op1=ALU.mult))
                done(dve.scalar_tensor_tensor(out=t["fine"][:, :, :], in0=sums, scalar=SUM_HIGH * WSCALE,
                                              in1=t["fine"][:, :, :], op0=ALU.is_le, op1=ALU.mult))

            def check(v):
                dve.wait_ge(out_ready, v + 1)
                done(dve.tensor_reduce(t["o_total"][:, :], t["o_tile"][v % 2][:, :, :], AX.XY, ALU.add))
                done(dve.scalar_tensor_tensor(out=t["finite"][:, :], in0=t["o_total"][:, :], scalar=OUT_HIGH,
                                              in1=t["finite"][:, :], op0=ALU.is_le, op1=ALU.mult))
                dve.scalar_tensor_tensor(out=t["finite"][:, :], in0=t["o_total"][:, :], scalar=-OUT_HIGH,
                                         in1=t["finite"][:, :], op0=ALU.is_ge, op1=ALU.mult).then_inc(checked, 1)

            for s in range(jobs.slots):
                if attend:
                    low_probabilities(s)
                for j in jobs.ends.get(s - 1 if attend else s, []):
                    job_low(j)
                if attend and s > LAG + 2 and (s - LAG - 2) % SLOTS == 0:
                    invert((s - LAG - 2) // SLOTS - 1)
                if attend and s > LAG + 8 and (s - LAG - 8) % SLOTS == 0:
                    check((s - LAG - 8) // SLOTS - 1)
            if attend:
                for j in jobs.ends.get(jobs.slots - 1, []):
                    job_low(j)
                invert(units[-1])
                check(units[-1])

        @block.gpsimd
        def _(pool):
            out_done = Steps(pool, out_step)

            def context_low(p):
                n, c, h = piece[p]
                a, b = HALVES[h]
                pool.wait_ge(ctx_high, p + 1)
                pool.tensor_tensor(t["ctx"][loads[n][1]][:, 1, c, a:b], t["ctx_raw"][p % 2][:, 0:b - a],
                                   t["ctx"][loads[n][1]][:, 0, c, a:b], ALU.subtract).then_inc(ctx_split, 1)

            def normalise(v):
                sums, out = t["o_sums"][v % 2], t["o_tile"][v % 2]
                heads = out[:, :, :].rearrange("p q (j d) -> p j q d", d=DH)
                pool.wait_ge(out_copied, HB * (v + 1))
                if v >= 2:
                    pool.wait_ge(out_stored[v % 2], 16 * (v // 2))
                    pool.wait_ge(checked, v - 1)
                for j in range(HB):
                    last = pool.tensor_tensor(heads[:, j], sums[:, j, :, 0:DH], sums[:, j, :, DH:2 * DH], ALU.add)
                out_done(last)
                pool.wait_ge(inverted, v + 1)
                for j in range(HB):
                    last = pool.tensor_tensor(heads[:, j], heads[:, j],
                                              t["o_inv"][v % 2][:, j, :, None].to_broadcast([P, QT, DH]), ALU.mult)
                out_done(last)
                kb = v % NBLK
                pool.tensor_tensor(out[:, :, :], out[:, :, :],
                                   t["bv_row"][:, None, kb * P:(kb + 1) * P].to_broadcast([P, QT, P]),
                                   ALU.add).then_inc(out_ready, 1)

            if not attend:
                for p in range(len(piece)):
                    context_low(p)
            for s in range(jobs.slots if attend else 0):
                for p in slot_pieces(s):
                    context_low(p)
                if s > LAG + 2 and (s - LAG - 2) % SLOTS == 0:
                    normalise((s - LAG - 2) // SLOTS - 1)
            if attend:
                normalise(units[-1])


def attention(nc, t):
    with ExitStack() as held:
        sb = lambda name, shape, dt: sbuf(nc, held, name, shape, dt)
        t = dict(t)
        t["ctx"] = [sb(f"ctx{n}", [P, 2, CC, M], F16) for n in range(2)]
        t["v"] = [sb(f"v{n}", [P, KT, H, VC], F16) for n in range(2)]
        t["k_stack"] = [sb(f"k_stack{n}", [TERMS * DH, HB, M], F16) for n in range(2)]
        t["k_parts"] = sb("k_parts", [P, 2, M], F16)
        t["ctx_raw"] = [sb(f"ctx_raw{n}", [P, HALVES[0][1]], F32) for n in range(2)]
        t["p"] = [sb(f"p{n}", [P, GROUP * N], F32) for n in range(NP)]
        t["p_low"] = [sb(f"p_low{n}", [P, GROUP * N], F16) for n in range(NP)]
        t["q_stack"] = [sb(f"q_stack{n}", [TERMS * DH, HB, N], F16) for n in range(2)]
        t["o_sums"] = [sb(f"o_sums{n}", [P, HB, QT, VC], F32) for n in range(2)]
        t["o_inv"] = [sb(f"o_inv{n}", [P, HB, QT], F32) for n in range(2)]
        t["o_tile"] = [sb(f"o_tile{n}", [P, QT, P], F32) for n in range(2)]
        t["o_total"] = sb("o_total", [P, 1], F32)
        t["ps_s"] = [held.enter_context(nc.psum_tensor(f"ps_s{n}", [P, GROUP * N], F32)) for n in range(2)]
        t["ps_o"] = banks(nc, held, ["ps_o0", "ps_o1"])
        t["ps_p"] = banks(nc, held, ["ps_p0", "ps_p1"])
        with phase(nc) as (block, sem):
            @block.vector
            def _(dve):
                for n in range(2):
                    dve.memset(t["v"][n][:, :, :, 2 * DH], WSCALE)
                dve.memset(t["fine"][:, :, :], 1.0)
                dve.memset(t["finite"][:, :], 1.0)

        attention_pass(nc, t, 0, [-1], attend=False, last=False, loads=[(-1, 0, 0), (-1, 1, 1)])
        units = list(range(2 * NBLK))
        with nc.Fori(0, B // 2 - 1) as i:
            attention_pass(nc, t, i, units, attend=True, last=False,
                           loads=[(NBLK - 1, 0, 2 * i + 2), (2 * NBLK - 1, 1, 2 * i + 3)])
        attention_pass(nc, t, B // 2 - 1, units, attend=True, last=True, loads=[])


def judge_range(nc, k, t):
    with ExitStack() as held, phase(nc) as (block, sem):
        worst = sbuf(nc, held, "j_worst", [P, 1], F32)
        fit = sbuf(nc, held, "j_fit", [P, 1], F32)
        ps = banks(nc, held, ["j_ps"])[0]
        step, ready, summed = sem("j_step"), sem("j_ready"), sem("j_summed")

        @block.vector
        def _(dve):
            done = Steps(dve, step)
            done(dve.tensor_reduce(worst[:, :], t["fine"][:, :, :], AX.XY, ALU.min))
            dve.tensor_tensor(fit[:, :], worst[:, :], t["finite"][:, :], ALU.mult).then_inc(ready, 1)
            dve.wait_ge(summed, 1)
            dve.tensor_scalar(t["unfit"][:, :], ps[0:1, 0:1], float(P) - 0.5, None, ALU.is_lt)

        @block.tensor
        def _(pe):
            pe.wait_ge(ready, 1)
            pe.matmul(ps[0:1, 0:1], fit[:, :], k["ones"][:, 0:1], start=True, stop=True).then_inc(summed, 1)


def attention_with_maximum(nc, k, t):
    ROUNDS = [range(0, 8), range(8, KT)]
    with ExitStack() as held:
        sb = lambda name, shape: sbuf(nc, held, "g_" + name, shape, F32)
        ctx = sb("ctx", [P, CC, M])
        w = sb("w", [P, 2, CC, P])
        bk = sb("bk", [P, 1])
        bv = sb("bv", [P, P])
        q = sb("q", [P, QT, P])
        q_t = sb("q_t", [P, N])
        k_t = sb("k_t", [P, M])
        v = sb("v", [P, KT, P])
        prob = sb("prob", [P, M])
        prob_t = sb("prob_t", [P, KT, P])
        top, total, inv = sb("top", [P, 1]), sb("total", [P, 1]), sb("inv", [P, 1])
        out = sb("out", [P, QT, P])
        ps_s = held.enter_context(nc.psum_tensor("g_ps_s", [P, 2048], F32))
        ps_t = held.enter_context(nc.psum_tensor("g_ps_t", [P, 1024], F32))
        ps_p, ps_o = banks(nc, held, ["g_ps_p", "g_ps_o"])
        with nc.Fori(0, B) as b, nc.Fori(0, NBLK) as kb, phase(nc) as (block, sem):
            (loaded, q_turned, q_copied, projected, taken, scored, topped, raised, turned, copied, weighed, normed,
             biased, step, stored) = (
                sem("g_" + n) for n in
                ("loaded", "q_turned", "q_copied", "projected", "taken", "scored", "topped", "raised", "turned",
                 "copied", "weighed", "normed", "biased", "step", "stored"))
            STEPS = [(j, n) for j in range(HB) for n in range(QT)]
            scale = float(DH) ** -0.5

            @block.sync
            def _(sp):
                sp.dma_start(ctx[:, :, :], t["ctx_t"][bass.ds(b, 1), :, :].rearrange("a (c p) n -> p (a c) n", p=P)).then_inc(loaded, 16)
                for n in range(2):
                    sp.dma_start(w[:, n, :, :], t["wkv_t"][:, bass.ds(kb * P + n * C, P)].rearrange("(c p) f -> p c f", p=P)).then_inc(loaded, 16)
                with nc.allow_non_contiguous_dma(reason="one bias for each partition"):
                    sp.dma_start(bk[:, :], t["bkv"][bass.ds(kb * P, P)].rearrange("(p a) -> p a", a=1)).then_inc(loaded, 16)
                sp.dma_start(bv[:, :], t["bkv"][bass.ds(kb * P + C, P)][None, :].to_broadcast([P, P])).then_inc(loaded, 16)
                sp.dma_start(q[:, :, :], t["q_nat"][bass.ds(b * N, N), bass.ds(kb * P, P)].rearrange("(t p) c -> p t c", p=P)).then_inc(loaded, 16)
                sp.wait_ge(biased, 1)
                sp.dma_start(t["o"][bass.ds(b * N, N), bass.ds(kb * P, P)].rearrange("(t p) c -> p t c", p=P), out[:, :, :]).then_inc(stored, 16)
                sp.wait_ge(stored, 16)

            @block.tensor
            def _(pe):
                pe.wait_ge(loaded, 96)
                for n in range(QT):
                    last = pe.transpose(ps_o[:, n * P:(n + 1) * P], q[:, n, :], k["id32"][:, :])
                last.then_inc(q_turned, 1)
                for n in range(4):
                    a, e = KEY_CUTS[n], KEY_CUTS[n + 1]
                    if n > 0:
                        pe.wait_ge(taken, n)
                    for c in range(CC):
                        last = pe.matmul(ps_p[:, 0:e - a], w[:, 0, c, :], ctx[:, c, a:e], start=(c == 0), stop=(c == CC - 1))
                    last.then_inc(projected, 1)
                for n in range(KT):
                    r = rows_of(n)
                    pe.wait_ge(taken, n + 4)
                    for c in range(CC):
                        last = pe.matmul(ps_p[0:r, 0:P], ctx[:, c, n * P:n * P + r], w[:, 1, c, :], start=(c == 0), stop=(c == CC - 1))
                    last.then_inc(projected, 1)
                pe.wait_ge(taken, KT + 4)
                pe.wait_ge(q_copied, 1)
                for i, (j, n) in enumerate(STEPS):
                    if i > 0:
                        pe.wait_ge(raised, i)
                    for a in range(0, M, 512):
                        e = min(a + 512, M)
                        last = pe.matmul(ps_s[:, a:e], q_t[j * DH:(j + 1) * DH, n * P:(n + 1) * P],
                                         k_t[j * DH:(j + 1) * DH, a:e], start=True, stop=True)
                    last.then_inc(scored, 1)
                    pe.wait_ge(raised, i + 1)
                    for m, tiles in enumerate(ROUNDS):
                        if i > 0 or m > 0:
                            pe.wait_ge(copied, 2 * i + m)
                        for x, kt in enumerate(tiles):
                            r = rows_of(kt)
                            last = pe.transpose(ps_t[0:r, x * P:(x + 1) * P], prob[:, kt * P:kt * P + r], k["id32"][:, :])
                        last.then_inc(turned, 1)
                    pe.wait_ge(copied, 2 * i + 2)
                    if i > 0:
                        pe.wait_ge(normed, i)
                    for kt in range(KT):
                        r = rows_of(kt)
                        last = pe.matmul(ps_o[:, 0:DH], prob_t[0:r, kt, :], v[0:r, kt, j * DH:(j + 1) * DH],
                                         start=(kt == 0), stop=(kt == KT - 1))
                    last.then_inc(weighed, 1)

            @block.scalar
            def _(act):
                for i in range(len(STEPS)):
                    act.wait_ge(topped, i + 1)
                    if i > 0:
                        act.wait_ge(turned, 2 * i)
                        act.wait_ge(normed, i)
                    act.activation(prob[:, :], ps_s[:, 0:M], ACT.Exp, bias=top[:, 0:1], scale=scale,
                                   accum_out=total[:, 0:1]).then_inc(raised, 1)

            @block.vector
            def _(dve):
                done = Steps(dve, step)
                dve.wait_ge(q_turned, 1)
                dve.tensor_copy(q_t[:, :], ps_o[:, :]).then_inc(q_copied, 1)
                for n in range(4):
                    a, e = KEY_CUTS[n], KEY_CUTS[n + 1]
                    dve.wait_ge(projected, n + 1)
                    dve.tensor_scalar(k_t[:, a:e], ps_p[:, 0:e - a], bk[:, 0:1], None, ALU.add).then_inc(taken, 1)
                for n in range(KT):
                    r = rows_of(n)
                    dve.wait_ge(projected, n + 5)
                    dve.tensor_copy(v[0:r, n, :], ps_p[0:r, 0:P]).then_inc(taken, 1)
                for i, (j, n) in enumerate(STEPS):
                    dve.wait_ge(scored, i + 1)
                    if i > 0:
                        dve.wait_ge(raised, i)
                    done(dve.tensor_reduce(top[:, :], ps_s[:, 0:M], AX.X, ALU.max))
                    dve.tensor_scalar(top[:, :], top[:, :], -scale, None, ALU.mult).then_inc(topped, 1)
                    for m, tiles in enumerate(ROUNDS):
                        dve.wait_ge(turned, 2 * i + m + 1)
                        if m == 0 and i > 0:
                            dve.wait_ge(weighed, i)
                        whole = [kt for kt in tiles if rows_of(kt) == P]
                        cols = len(whole) * P
                        last = dve.tensor_copy(prob_t[:, whole[0]:whole[-1] + 1, :],
                                               ps_t[:, 0:cols].rearrange("p (n q) -> p n q", q=P))
                        if len(whole) < len(tiles):
                            last = dve.tensor_copy(prob_t[0:TAIL, KT - 1, :], ps_t[0:TAIL, cols:cols + P])
                        last.then_inc(copied, 1)
                    dve.wait_ge(raised, i + 1)
                    done(dve.reciprocal(inv[:, :], total[:, :]))
                    dve.wait_ge(weighed, i + 1)
                    dve.tensor_scalar(out[:, n, j * DH:(j + 1) * DH], ps_o[:, 0:DH], inv[:, 0:1], None,
                                      ALU.mult).then_inc(normed, 1)
                dve.wait_ge(normed, len(STEPS))
                dve.tensor_tensor(out[:, :, :], out[:, :, :], bv[:, None, :].to_broadcast([P, QT, P]),
                                  ALU.add).then_inc(biased, 1)


def project_outputs(nc, k, t):
    with ExitStack() as held:
        sb = lambda name, shape, dt: sbuf(nc, held, "u_" + name, shape, dt)
        o, xin, oy = (sb(n, [P, QT, C], F32) for n in ("o", "xin", "oy"))
        oq = sb("oq", [P, QT, C], BF16)
        oqt = sb("oqt", [P, CC, N], BF16)
        x2 = sb("x2", [P, QT, C], F32)
        xn = sb("xn", [P, QT, C], F32)
        parts = sb("parts", [P, QT, 2, C], F16)
        parts_t = sb("parts_t", [P, 2, CC, N], F16)
        pair = sb("pair", [P, QT, 2 * E], F32)
        st = sb("st", [P, QT, 6], F32)
        mv = sb("mv", [P, QT, 2], F32)
        amax, so, inv, std, rstd, tmp, shift = (
            sb(n, [P, QT], F32) for n in ("amax", "so", "inv", "std", "rstd", "tmp", "shift"))
        ps_y = banks(nc, held, [f"u_py{n}" for n in range(QT)])
        ps_b = banks(nc, held, ["u_pb0", "u_pb1"], BF16)
        ps_t = [b[:, :].bitcast(F16) for b in ps_b]
        ps_g = banks(nc, held, ["u_pg"])[0]
        with nc.Fori(0, B) as b, phase(nc) as (block, sem):
            (o_in, x_in, step, quantized, turned, copied, projected, biased, scaled, x2_ready, measured, rooted,
             normed, high, split, xn_turned, xn_copied, gated, stored) = (
                sem("u_" + n) for n in
                ("o_in", "x_in", "step", "quantized", "turned", "copied", "projected", "biased", "scaled", "x2_ready",
                 "measured", "rooted", "normed", "high", "split", "xn_turned", "xn_copied", "gated", "stored"))

            @block.sync
            def _(sp):
                rows = lambda a: a[bass.ds(b * N, N), :].rearrange("(t p) c -> p t c", p=P)
                sp.dma_start(o[:, :, :], rows(t["o"])).then_inc(o_in, 16)
                sp.dma_start(xin[:, :, :], rows(t["x"])).then_inc(x_in, 16)
                sp.wait_ge(x2_ready, QT)
                sp.dma_start(rows(t["x2"]), x2[:, :, :]).then_inc(stored, 16)
                sp.wait_ge(split, 1)
                sp.dma_start(t["xn"][:, bass.ds(b * QT, QT), :],
                             parts[:, :, :, :].rearrange("p t s c -> p t (s c)")).then_inc(stored, 16)
                sp.wait_ge(stored, 32)

            @block.gpsimd
            def _(pool):
                pool.wait_ge(x_in, 16)
                pool.tensor_tensor(xin[:, :, :], xin[:, :, :], t["bp_row"][:, None, :].to_broadcast([P, QT, C]),
                                   ALU.add).then_inc(biased, 1)
                pool.wait_ge(biased, 1)
                for n in range(QT):
                    pool.wait_ge(scaled, n + 1)
                    pool.tensor_tensor(x2[:, n, :], xn[:, n, :], xin[:, n, :], ALU.add).then_inc(x2_ready, 1)

            @block.scalar
            def _(act):
                for half in range(2):
                    act.wait_ge(turned, half + 1)
                    act.copy(oqt[:, 2 * half:2 * half + 2, :],
                             ps_b[half][:, :].rearrange("p (c n) -> p c n", c=2)).then_inc(copied, 1)
                act.wait_ge(measured, 1)
                act.activation(std[:, :], mv[:, :, 1], ACT.Sqrt, bias=k["eps"][:, 0:1]).then_inc(rooted, 1)
                act.wait_ge(measured, 2)
                for n in range(QT):
                    last = act.activation(xn[:, n, :], x2[:, n, :], ACT.Identity, bias=shift[:, n:n + 1],
                                          scale=rstd[:, n:n + 1])
                last.then_inc(normed, 1)
                act.wait_ge(normed, 1)
                act.copy(parts[:, :, 0, :], xn[:, :, :]).then_inc(high, 1)
                for g in range(4):
                    act.wait_ge(xn_turned, g + 1)
                    act.copy(parts_t[:, g // 2, 2 * (g % 2):2 * (g % 2) + 2, :],
                             ps_t[g % 2].rearrange("p (c n) -> p c n", c=2)).then_inc(xn_copied, 1)

            @block.vector
            def _(dve):
                done = Steps(dve, step)
                dve.wait_ge(o_in, 16)
                done(dve.tensor_reduce(amax[:, :], o[:, :, :], AX.X, ALU.max, apply_absolute_value=True))
                done(dve.tensor_scalar(so[:, :], amax[:, :], 1.0 / QMAX, 1e-8, ALU.mult, ALU.max))
                done(dve.reciprocal(inv[:, :], so[:, :]))
                for n in range(QT):
                    last = dve.tensor_scalar(oy[:, n, :], o[:, n, :], inv[:, n:n + 1], QMAX, ALU.mult, ALU.min)
                done(last)
                done(dve.tensor_scalar(o[:, :, :], oy[:, :, :], -QMAX, ROUND, ALU.max, ALU.add))
                dve.tensor_scalar(oq[:, :, :], o[:, :, :], ROUND, None, ALU.subtract).then_inc(quantized, 1)
                for n in range(QT):
                    dve.wait_ge(projected, n + 1)
                    dve.scalar_tensor_tensor(out=xn[:, n, :], in0=ps_y[n][:, :], scalar=so[:, n:n + 1],
                                             in1=t["sp_row"][:, :], op0=ALU.mult, op1=ALU.mult).then_inc(scaled, 1)
                for n in range(QT):
                    dve.wait_ge(x2_ready, n + 1)
                    last = dve.bn_stats(st[:, n, :], x2[:, n, :])
                done(last)
                for n in range(QT):
                    last = dve.bn_aggr(mv[:, n, :], st[:, n, :])
                last.then_inc(measured, 1)
                dve.wait_ge(rooted, 1)
                inverse_std(dve, done, mv[:, :, 1], std[:, :], rstd[:, :], tmp[:, :])
                dve.scalar_tensor_tensor(out=shift[:, :], in0=mv[:, :, 0], scalar=-1.0, in1=rstd[:, :],
                                         op0=ALU.mult, op1=ALU.mult).then_inc(measured, 1)
                dve.wait_ge(high, 1)
                dve.tensor_tensor(parts[:, :, 1, :], xn[:, :, :], parts[:, :, 0, :], ALU.subtract).then_inc(split, 1)
                dve.wait_ge(gated, 1)
                done(dve.tensor_copy(pair[:, :, :], ps_g[:, 0:QT * 2 * E].rearrange("p (t e) -> p t e", t=QT)))
                dve.tensor_tensor(t["logits"][:, bass.ds(b * QT, QT), :], pair[:, :, 0:E], pair[:, :, E:2 * E], ALU.add)

            @block.tensor
            def _(pe):
                pe.wait_ge(quantized, 1)
                for half in range(2):
                    for c in range(2 * half, 2 * half + 2):
                        for n in range(QT):
                            at = (c % 2) * N + n * P
                            last = pe.transpose(ps_b[half][:, at:at + P], oq[:, n, c * P:(c + 1) * P], k["idb"][:, :])
                    last.then_inc(turned, 1)
                pe.wait_ge(copied, 2)
                for n in range(QT):
                    for c in range(CC):
                        last = pe.matmul(ps_y[n][:, :], oqt[:, c, n * P:(n + 1) * P], t["wp_t"][:, c, :],
                                         start=(c == 0), stop=(c == CC - 1))
                    last.then_inc(projected, 1)
                for g in range(4):
                    if g == 0:
                        pe.wait_ge(high, 1)
                    if g == 2:
                        pe.wait_ge(split, 1)
                    if g >= 2:
                        pe.wait_ge(xn_copied, g - 1)
                    for c in range(2 * (g % 2), 2 * (g % 2) + 2):
                        for n in range(QT):
                            at = (c % 2) * N + n * P
                            last = pe.transpose(ps_t[g % 2][:, at:at + P], parts[:, n, g // 2, c * P:(c + 1) * P],
                                                k["id16"][:, :])
                    last.then_inc(xn_turned, 1)
                pe.wait_ge(xn_copied, 4)
                for n in range(QT):
                    for part in range(2):
                        for c in range(CC):
                            last = pe.matmul(ps_g[:, n * 2 * E:(n + 1) * 2 * E],
                                             parts_t[:, part, c, n * P:(n + 1) * P], t["gate"][:, c, :],
                                             start=(part == 0 and c == 0), stop=(part == 1 and c == CC - 1))
                last.then_inc(gated, 1)


TT = B * N // P
TILES = 72
assert TILES * P >= B * N * TOPK + E * (P - 1)


def route(nc, k, t):
    with ExitStack() as held, phase(nc) as (block, sem):
        sb = lambda name, shape, dt=F32: sbuf(nc, held, "r_" + name, shape, dt)
        best = sb("best", [P, TT, 8])
        index = sb("index", [P, TT, 8], U32)
        chosen = sb("chosen", [P, TOPK, TT])
        hot = sb("hot", [P, TOPK, TT, E])
        any_hot = sb("any_hot", [P, TT, E])
        any_hot_b = sb("any_hot_b", [P, TT, E], BF16)
        total, sum_a, sum_b, place = (sb(n, [P, TT, E]) for n in ("total", "sum_a", "sum_b", "place"))
        picked = sb("picked", [P, TOPK, TT, E])
        tiles, ends, ends_b, starts, base = (sb(n, [P, E]) for n in ("tiles", "ends", "ends_b", "starts", "base"))
        gap, ratio, first = (sb(n, [P, TT]) for n in ("gap", "ratio", "first"))
        pos = sb("pos", [P, TOPK, TT])
        experts_i = sb("experts_i", [P, E], I32)
        experts = sb("experts", [P, E])
        tile_i = sb("tile_i", [1, TILES], I32)
        tile_f = sb("tile_f", [1, TILES])
        passed = sb("passed", [1, TILES, E])
        of_tile = sb("of_tile", [1, TILES])
        before = sb("before", [P, P])
        before_b = sb("before_b", [P, P], BF16)
        ones_b = sb("ones_b", [P, P], BF16)
        ps_before, ps_total = banks(nc, held, ["r_pb", "r_pt"])
        made, step, hot_ready, summed, gap_ready, ratio_ready, routed = (
            sem("r_" + n) for n in ("made", "step", "hot_ready", "summed", "gap_ready", "ratio_ready", "routed"))
        stored, fetched = sem("r_stored"), sem("r_fetched")

        @block.gpsimd
        def _(pool):
            pool.iota(experts_i[:, :], [[1, E]], base=0, channel_multiplier=0)
            pool.iota(tile_i[:, :], [[1, TILES]], base=0, channel_multiplier=0)
            pool.affine_select(out=before[:, :], in_=k["ones"][:, :], compare_op=ALU.is_gt, fill=0.0, base=0,
                               pattern=[[1, P]], channel_multiplier=-1).then_inc(made, 1)
            for n in range(TT):
                for c in range(TOPK):
                    if n == 0 and c == 0:
                        pool.wait_ge(routed, 1)
                        pool.wait_ge(t["zeroed"], 16)
                    pool.indirect_dma_start(
                        out=t["xs"][:, :], out_offset=bass.IndirectOffsetOnAxis(ap=t["rows"][:, c, n:n + 1], axis=0),
                        in_=t["xn"][:, n, :], in_offset=None).then_inc(stored, 16)
            pool.wait_ge(stored, 16 * TT * TOPK)

        @block.scalar
        def _(act):
            act.wait_ge(gap_ready, 1)
            act.activation(ratio[:, :], gap[:, :], ACT.Exp, scale=1.0 / WSCALE).then_inc(ratio_ready, 1)

        @block.tensor
        def _(pe):
            pe.wait_ge(hot_ready, 1)
            flat = any_hot_b[:, :, :].rearrange("p t e -> p (t e)")
            pe.matmul(ps_before[:, 0:TT * E], before_b[:, :], flat, start=True, stop=True)
            pe.matmul(ps_total[:, 0:TT * E], ones_b[:, :], flat, start=True, stop=True).then_inc(summed, 1)

        @block.vector
        def _(dve):
            done = Steps(dve, step)
            for n in range(TT):
                last = dve.max(best[:, n, :], t["logits"][:, n, :])
            done(last)
            for n in range(TT):
                last = dve.max_index(index[:, n, :], best[:, n, :], t["logits"][:, n, :])
            done(last)
            dve.tensor_tensor(gap[:, :], best[:, :, 1], best[:, :, 0], ALU.subtract).then_inc(gap_ready, 1)
            dve.wait_ge(made, 1)
            dve.tensor_copy(experts[:, :], experts_i[:, :])
            dve.tensor_copy(before_b[:, :], before[:, :])
            dve.memset(ones_b[:, :], 1.0)
            dve.tensor_copy(tile_f[:, :], tile_i[:, :])
            done(dve.tensor_copy(chosen[:, :, :], index[:, :, 0:TOPK].rearrange("p t c -> p c t")))
            for c in range(TOPK):
                last = dve.tensor_tensor(hot[:, c, :, :], experts[:, None, :].to_broadcast([P, TT, E]),
                                         chosen[:, c, :, None].to_broadcast([P, TT, E]), ALU.is_equal)
            done(last)
            done(dve.tensor_tensor(any_hot[:, :, :], hot[:, 0, :, :], hot[:, 1, :, :], ALU.add))
            dve.tensor_copy(any_hot_b[:, :, :], any_hot[:, :, :]).then_inc(hot_ready, 1)
            dve.wait_ge(summed, 1)
            flat = lambda a: a[:, :, :].rearrange("p t e -> p (t e)")
            dve.tensor_copy(flat(total), ps_total[:, 0:TT * E])
            done(dve.tensor_copy(flat(sum_a), ps_total[:, 0:TT * E]))
            src, dst = sum_a, sum_b
            for by in (1, 2, 4, 8, 16):
                dve.tensor_copy(dst[:, 0:by, :], src[:, 0:by, :])
                done(dve.tensor_tensor(dst[:, by:, :], src[:, by:, :], src[:, 0:TT - by, :], ALU.add))
                src, dst = dst, src
            done(dve.tensor_scalar(tiles[:, :], src[:, TT - 1, :], float(P - 1), 1.0 / P, ALU.add, ALU.mult))
            done(dve.tensor_scalar(tiles[:, :], tiles[:, :], -0.5 + 0.25 / P, ROUND, ALU.add, ALU.add))
            done(dve.tensor_scalar(tiles[:, :], tiles[:, :], ROUND, None, ALU.subtract))
            done(dve.tensor_copy(ends[:, :], tiles[:, :]))
            e_src, e_dst = ends, ends_b
            for by in (1, 2, 4):
                dve.tensor_copy(e_dst[:, 0:by], e_src[:, 0:by])
                done(dve.tensor_tensor(e_dst[:, by:], e_src[:, by:], e_src[:, 0:E - by], ALU.add))
                e_src, e_dst = e_dst, e_src
            done(dve.tensor_tensor(starts[:, :], e_src[:, :], tiles[:, :], ALU.subtract))
            done(dve.tensor_scalar(base[:, :], starts[:, :], float(P), None, ALU.mult))
            done(dve.tensor_tensor(place[:, :, :], src[:, :, :], total[:, :, :], ALU.subtract))
            done(dve.tensor_tensor(place[:, :, :], place[:, :, :], base[:, None, :].to_broadcast([P, TT, E]), ALU.add))
            done(dve.tensor_tensor(flat(place), flat(place), ps_before[:, 0:TT * E], ALU.add))
            for c in range(TOPK):
                last = dve.tensor_tensor(picked[:, c, :, :], hot[:, c, :, :], place[:, :, :], ALU.mult)
            done(last)
            done(dve.tensor_reduce(pos[:, :, :], picked[:, :, :, :], AX.X, ALU.add))
            dve.tensor_copy(t["rows"][:, :, :], pos[:, :, :]).then_inc(routed, 1)
            done(dve.tensor_tensor(passed[:, :, :], tile_f[:, :, None].to_broadcast([1, TILES, E]),
                                   starts[0:1, None, :].to_broadcast([1, TILES, E]), ALU.is_ge))
            done(dve.tensor_reduce(of_tile[:, :], passed[:, :, :], AX.X, ALU.add))
            done(dve.tensor_scalar(of_tile[:, :], of_tile[:, :], -1.0, None, ALU.add))
            dve.tensor_copy(t["expert_of"][:, :], of_tile[:, :])
            dve.wait_ge(ratio_ready, 1)
            done(dve.tensor_scalar(first[:, :], ratio[:, :], 1.0, None, ALU.add))
            done(dve.reciprocal(first[:, :], first[:, :]))
            dve.tensor_scalar(t["weights"][:, 0, :], first[:, :], 1.0 / WSCALE, None, ALU.mult)
            dve.scalar_tensor_tensor(out=t["weights"][:, 1, :], in0=ratio[:, :], scalar=1.0 / WSCALE,
                                     in1=first[:, :], op0=ALU.mult, op1=ALU.mult)


def split_expert_weights(nc, t):
    with ExitStack() as held, phase(nc) as (block, sem):
        raw_i = [sbuf(nc, held, f"e_raw_i{n}", [P, CC, 2 * FF], F32) for n in range(2)]
        raw_o = [sbuf(nc, held, f"e_raw_o{n}", [P, FF // P, C], F32) for n in range(2)]
        loaded = [sem(f"e_loaded{n}") for n in range(2)]
        high, split = sem("e_high"), sem("e_split")

        @block.sync
        def _(sp):
            for e in range(E):
                if e >= 2:
                    sp.wait_ge(split, 2 * (e - 1))
                for n, w in enumerate((t["wi_0"], t["wi_1"])):
                    sp.dma_start(raw_i[e % 2][:, :, n * FF:(n + 1) * FF],
                                 w[e].rearrange("(c p) f -> p c f", p=P)).then_inc(loaded[e % 2], 16)
                sp.dma_start(raw_o[e % 2][:, :, :], t["w_out"][e].rearrange("(m p) c -> p m c", p=P)).then_inc(loaded[e % 2], 16)

        @block.scalar
        def _(act):
            for e in range(E):
                act.wait_ge(loaded[e % 2], 48 * (e // 2 + 1))
                act.mul(t["wi"][:, e, 0, :, :], raw_i[e % 2][:, :, :], WSCALE).then_inc(high, 1)
                act.mul(t["wo"][:, e, 0, :, :], raw_o[e % 2][:, :, :], WSCALE).then_inc(high, 1)

        @block.vector
        def _(dve):
            for e in range(E):
                for n, (whole, parts) in enumerate(((raw_i, t["wi"]), (raw_o, t["wo"]))):
                    dve.wait_ge(high, 2 * e + n + 1)
                    flat = lambda a: a.rearrange("p a b -> p (a b)")
                    dve.scalar_tensor_tensor(out=flat(parts[:, e, 1, :, :]), in0=flat(whole[e % 2][:, :, :]),
                                             scalar=WSCALE, in1=flat(parts[:, e, 0, :, :]), op0=ALU.mult,
                                             op1=ALU.subtract).then_inc(split, 1)


RUN = 12
MB = FF // P


def run_experts(nc, k, t):
    with ExitStack() as held:
        sb = lambda name, shape, dt: sbuf(nc, held, "f_" + name, shape, dt)
        xs = [sb(f"xs{n}", [P, 2 * C], F16) for n in range(3)]
        xt = [sb(f"xt{n}", [P, 2, CC, P], F16) for n in range(2)]
        gate = [sb(f"gate{n}", [P, FF], F32) for n in range(2)]
        inner = [sb(f"inner{n}", [P, FF], F32) for n in range(2)]
        parts = [sb(f"parts{n}", [P, 2, FF], F16) for n in range(2)]
        it = [sb(f"it{n}", [P, 2, MB, P], F16) for n in range(2)]
        y = [sb(f"y{n}", [P, C], F32) for n in range(2)]
        ps_x = banks(nc, held, ["f_px0", "f_px1"], F16)
        ps_h = banks(nc, held, ["f_ph0", "f_ph1"])
        ps_i = banks(nc, held, ["f_pi0", "f_pi1"], F16)
        ps_y = banks(nc, held, ["f_py0", "f_py1"])
        with nc.Fori(0, TILES // RUN) as i, phase(nc) as (block, sem):
            x_in = [sem(f"f_x_in{n}") for n in range(3)]
            y_out = [sem(f"f_y_out{n}") for n in range(2)]
            x_turned, x_copied, hidden, gated, multiplied, high, split, i_turned, i_copied, produced, y_ready = (
                sem("f_" + n) for n in ("x_turned", "x_copied", "hidden", "gated", "multiplied", "high", "split",
                                        "i_turned", "i_copied", "produced", "y_ready"))

            @block.sync
            def _(sp):
                def store(n):
                    sp.wait_ge(y_ready, n + 1)
                    sp.dma_start(t["ys"][bass.ds(i * (RUN * P) + n * P, P), :], y[n % 2][:, :]).then_inc(y_out[n % 2], 16)

                for n in range(RUN + 3):
                    if n < RUN:
                        if n >= 3:
                            sp.wait_ge(x_turned, n - 2)
                        sp.dma_start(xs[n % 3][:, :], t["xs"][bass.ds(i * (RUN * P) + n * P, P), :]).then_inc(x_in[n % 3], 16)
                    if n >= 3:
                        store(n - 3)
                for n in range(2):
                    sp.wait_ge(y_out[n], 16 * (RUN // 2))

            @block.tensor
            def _(pe):
                def turn_x(n):
                    pe.wait_ge(x_in[n % 3], 16 * (n // 3 + 1))
                    if n >= 2:
                        pe.wait_ge(x_copied, n - 1)
                    for b in range(2 * CC):
                        last = pe.transpose(ps_x[n % 2][:, b * P:(b + 1) * P], xs[n % 3][:, b * P:(b + 1) * P],
                                            k["id16"][:, :])
                    last.then_inc(x_turned, 1)

                def hide(n, e):
                    pe.wait_ge(x_copied, n + 1)
                    if n >= 2:
                        pe.wait_ge(multiplied, n - 1)
                    for m in range(TERMS * CC):
                        c, term = m // TERMS, m % TERMS
                        x_part, w_part = (0, 1, 0)[term], (0, 0, 1)[term]
                        last = pe.matmul(ps_h[n % 2][:, :], xt[n % 2][:, x_part, c, :],
                                         t["wi"][:, bass.ds(e, 1), w_part, c, :].rearrange("p a f -> p (a f)"),
                                         start=(m == 0), stop=(m == TERMS * CC - 1))
                    last.then_inc(hidden, 1)

                def turn_inner(n):
                    pe.wait_ge(split, n + 1)
                    if n >= 2:
                        pe.wait_ge(i_copied, n - 1)
                    for part in range(2):
                        for m in range(MB):
                            at = (part * MB + m) * P
                            last = pe.transpose(ps_i[n % 2][:, at:at + P], parts[n % 2][:, part, m * P:(m + 1) * P],
                                                k["id16"][:, :])
                    last.then_inc(i_turned, 1)

                def produce(n, e):
                    pe.wait_ge(i_copied, n + 1)
                    if n >= 2:
                        pe.wait_ge(y_ready, n - 1)
                    for m in range(TERMS * MB):
                        c, term = m // TERMS, m % TERMS
                        i_part, w_part = (0, 1, 0)[term], (0, 0, 1)[term]
                        last = pe.matmul(ps_y[n % 2][:, :], it[n % 2][:, i_part, c, :],
                                         t["wo"][:, bass.ds(e, 1), w_part, c, :].rearrange("p a f -> p (a f)"),
                                         start=(m == 0), stop=(m == TERMS * MB - 1))
                    last.then_inc(produced, 1)

                experts = {}
                turn_x(0)
                for n in range(RUN + 1):
                    if n < RUN:
                        experts[n] = pe.value_load(t["expert_of"][0:1, bass.ds(i * RUN + n, 1)], min_val=0, max_val=E - 1)
                        if n + 1 < RUN:
                            turn_x(n + 1)
                        hide(n, experts[n])
                    if n >= 1:
                        turn_inner(n - 1)
                        produce(n - 1, experts[n - 1])

            @block.scalar
            def _(act):
                def finish(n):
                    act.wait_ge(produced, n + 1)
                    if n >= 2:
                        act.wait_ge(y_out[n % 2], 16 * (n // 2))
                    act.copy(y[n % 2][:, :], ps_y[n % 2][:, :]).then_inc(y_ready, 1)

                for n in range(RUN):
                    act.wait_ge(hidden, n + 1)
                    act.activation(gate[n % 2][:, :], ps_h[n % 2][:, 0:FF], ACT.Silu, scale=1.0 / WSCALE).then_inc(gated, 1)
                    act.wait_ge(multiplied, n + 1)
                    act.copy(parts[n % 2][:, 0, :], inner[n % 2][:, :]).then_inc(high, 1)
                    if n >= 1:
                        finish(n - 1)
                finish(RUN - 1)

            @block.vector
            def _(dve):
                def copy_x(n):
                    dve.wait_ge(x_turned, n + 1)
                    if n >= 2:
                        dve.wait_ge(hidden, n - 1)
                    dve.tensor_copy(xt[n % 2][:, :, :, :].rearrange("p s c n -> p (s c n)"), ps_x[n % 2][:, :]).then_inc(x_copied, 1)

                copy_x(0)
                for n in range(RUN):
                    if n + 1 < RUN:
                        copy_x(n + 1)
                    dve.wait_ge(gated, n + 1)
                    dve.scalar_tensor_tensor(out=inner[n % 2][:, :], in0=ps_h[n % 2][:, FF:2 * FF],
                                             scalar=1.0 / WSCALE, in1=gate[n % 2][:, :], op0=ALU.mult,
                                             op1=ALU.mult).then_inc(multiplied, 1)
                    dve.wait_ge(high, n + 1)
                    dve.tensor_tensor(parts[n % 2][:, 1, :], inner[n % 2][:, :], parts[n % 2][:, 0, :],
                                      ALU.subtract).then_inc(split, 1)
                    dve.wait_ge(i_turned, n + 1)
                    if n >= 2:
                        dve.wait_ge(produced, n - 1)
                    dve.tensor_copy(it[n % 2][:, :, :, :].rearrange("p s m n -> p (s m n)"),
                                    ps_i[n % 2][:, 0:2 * MB * P]).then_inc(i_copied, 1)


def combine(nc, t):
    with ExitStack() as held, phase(nc) as (block, sem):
        NB = 4
        rows = [sbuf(nc, held, f"c_rows{n}", [P, TOPK, C], F32) for n in range(NB)]
        res = [sbuf(nc, held, f"c_res{n}", [P, C], F32) for n in range(NB)]
        x_in, y_in, out = ([sem(f"c_{x}{n}") for n in range(NB)] for x in ("x_in", "y_in", "out"))
        first, second = sem("c_first"), sem("c_second")

        @block.sync
        def _(sp):
            for n in range(TT):
                if n >= NB:
                    sp.wait_ge(out[n % NB], 16 * (n // NB))
                sp.dma_start(res[n % NB][:, :], t["x2"][n * P:(n + 1) * P, :]).then_inc(x_in[n % NB], 16)

        @block.gpsimd
        def _(pool):
            for n in range(TT):
                if n >= NB:
                    pool.wait_ge(second, n - NB + 1)
                for c in range(TOPK):
                    pool.indirect_dma_start(
                        out=rows[n % NB][:, c, :], out_offset=None, in_=t["ys"][:, :],
                        in_offset=bass.IndirectOffsetOnAxis(ap=t["rows"][:, c, n:n + 1], axis=0)).then_inc(y_in[n % NB], 16)

        @block.vector
        def _(dve):
            for n in range(TT):
                dve.wait_ge(x_in[n % NB], 16 * (n // NB + 1))
                dve.wait_ge(y_in[n % NB], 16 * TOPK * (n // NB + 1))
                dve.scalar_tensor_tensor(out=res[n % NB][:, :], in0=rows[n % NB][:, 0, :],
                                         scalar=t["weights"][:, 0, n:n + 1], in1=res[n % NB][:, :],
                                         op0=ALU.mult, op1=ALU.add).then_inc(first, 1)
                dve.wait_ge(first, n + 1)
                dve.scalar_tensor_tensor(out=res[n % NB][:, :], in0=rows[n % NB][:, 1, :],
                                         scalar=t["weights"][:, 1, n:n + 1], in1=res[n % NB][:, :],
                                         op0=ALU.mult, op1=ALU.add).then_inc(second, 1)

        @block.scalar
        def _(act):
            for n in range(TT):
                act.wait_ge(second, n + 1)
                act.dma_start(t["out"][n * P:(n + 1) * P, :], res[n % NB][:, :]).then_inc(out[n % NB], 16)
            for n in range(NB):
                act.wait_ge(out[n], 16 * (TT // NB))


def program(nc, x, ctx_t, wq, bq, wkv_t, bkv, wp, bp, w_gate, wi_0, wi_1, w_out, out):
    x = x.rearrange("b n c -> (b n) c")
    out = out.rearrange("b n c -> (b n) c")
    t = {"x": x, "out": out, "ctx_t": ctx_t, "wkv_t": wkv_t, "bkv": bkv, "wi_0": wi_0, "wi_1": wi_1, "w_out": w_out}
    for name, shape, dt in (
        ("q_nat", (B * N, C), F32),
        ("q_t", (2, NBLK, P, B * N), F16),
        ("o", (B * N, C), F32),
        ("x2", (B * N, C), F32),
        ("xs", (TILES * P, 2 * C), F16),
        ("ys", (TILES * P, C), F32),
    ):
        t[name] = nc.dram_tensor("d_" + name, shape, dt).ap()
    with ExitStack() as held:
        sb = lambda name, shape, dt=F32: sbuf(nc, held, name, shape, dt)
        k = make_constants(nc, held)
        k["eps"] = sb("eps", [P, 1])
        t["bk"], t["bv_row"] = sb("bk", [P, NBLK]), sb("bv_row", [P, C])
        t["fine"], t["finite"], t["unfit"] = sb("fine", [P, HB, QT]), sb("finite", [P, 1]), sb("unfit", [1, 1], I32)
        t["zeroed"] = held.enter_context(nc.semaphore("zeroed"))
        with ExitStack() as early:
            t["wkv"] = sbuf(nc, early, "wkv", [P, 2, CC, 2 * C], F16)
            with ExitStack() as first:
                wq_t = sbuf(nc, first, "wq_t", [P, CC, C], BF16)
                sq_row = sbuf(nc, first, "sq_row", [P, C], F32)
                bq_row = sbuf(nc, first, "bq_row", [P, C], F32)
                zero = sbuf(nc, first, "zero", [P, 2 * C], F16)
                with phase(nc) as (block, sem):
                    rows_in, cleared = sem("rows_in"), sem("cleared")

                    @block.sync
                    def _(sp):
                        sp.dma_start(bq_row[:, :], bq[None, :].to_broadcast([P, C])).then_inc(rows_in, 16)
                        sp.dma_start(t["bv_row"][:, :], bkv[C:2 * C][None, :].to_broadcast([P, C])).then_inc(rows_in, 16)
                        with nc.allow_non_contiguous_dma(reason="one bias for each partition"):
                            sp.dma_start(t["bk"][:, :], bkv[0:C].rearrange("(k p) -> p k", p=P)).then_inc(rows_in, 16)
                        sp.wait_ge(rows_in, 48)
                        sp.wait_ge(cleared, 1)
                        sp.dma_start(t["xs"].rearrange("(t p) c -> p t c", p=P),
                                     zero[:, None, :].to_broadcast([P, TILES, 2 * C])).then_inc(t["zeroed"], 16)

                    @block.vector
                    def _(dve):
                        dve.memset(k["eps"][:, :], EPS)
                        dve.memset(zero[:, :], 0.0).then_inc(cleared, 1)
                        dve.wait_ge(rows_in, 48)
                        dve.tensor_scalar(t["bk"][:, :], t["bk"][:, :], WSCALE, None, ALU.mult)

                quantize_weight(nc, k, "wq_", wq, wq_t, sq_row)
                split_kv_weight(nc, wkv_t, t["wkv"])
                project_queries(nc, k, x, wq_t, sq_row, bq_row, t["q_nat"], t["q_t"])
                with phase(nc) as (block, sem):
                    @block.sync
                    def _(sp):
                        sp.wait_ge(t["zeroed"], 16)
            attention(nc, t)
        judge_range(nc, k, t)
        unfit = nc.values_load(t["unfit"][0:1, 0:1], min_val=0, max_val=1)
        with nc.If(unfit > 0):
            attention_with_maximum(nc, k, t)

        t["bp_row"], t["sp_row"], t["wp_t"] = sb("bp_row", [P, C]), sb("sp_row", [P, C]), sb("wp_t", [P, CC, C], BF16)
        t["gate"], t["logits"] = sb("gate", [P, CC, 2 * E], F16), sb("logits", [P, TT, E])
        t["rows"], t["weights"] = sb("rows", [P, TOPK, TT], U32), sb("weights", [P, TOPK, TT])
        t["expert_of"] = sb("expert_of", [1, TILES], I32)
        gate_raw = sb("gate_raw", [P, CC, E])
        with phase(nc) as (block, sem):
            late_in, high = sem("late_in"), sem("gate_high")

            @block.sync
            def _(sp):
                sp.dma_start(t["bp_row"][:, :], bp[None, :].to_broadcast([P, C])).then_inc(late_in, 16)
                sp.dma_start(gate_raw[:, :, :], w_gate.rearrange("(c p) e -> p c e", p=P)).then_inc(late_in, 16)
                sp.wait_ge(late_in, 32)

            @block.vector
            def _(dve):
                dve.wait_ge(late_in, 32)
                dve.tensor_scalar(t["gate"][:, :, 0:E], gate_raw[:, :, :], WSCALE, None, ALU.mult).then_inc(high, 1)
                dve.wait_ge(high, 1)
                dve.scalar_tensor_tensor(out=t["gate"][:, :, E:2 * E], in0=gate_raw[:, :, :], scalar=WSCALE,
                                         in1=t["gate"][:, :, 0:E], op0=ALU.mult, op1=ALU.subtract)

        quantize_weight(nc, k, "wp_", wp, t["wp_t"], t["sp_row"])
        with ExitStack() as middle:
            t["xn"] = sbuf(nc, middle, "xn", [P, TT, 2 * C], F16)
            project_outputs(nc, k, t)
            route(nc, k, t)
        t["wi"] = sb("wi_parts", [P, E, 2, CC, 2 * FF], F16)
        t["wo"] = sb("wo_parts", [P, E, 2, MB, C], F16)
        split_expert_weights(nc, t)
        run_experts(nc, k, t)
        combine(nc, t)


def kernel(**inputs):
    import numpy as _np
    import concourse.bacc as _bacc
    from concourse import mybir as _mybir
    from concourse.bass_utils import run_bass_kernel_spmd as _run

    nc = _bacc.Bacc("TRN2", target_bir_lowering=False, num_devices=1)
    order = [("x", (0, 1, 2)), ("ctx_2048", (0, 2, 1)), ("L0_xattn_wq", (0, 1)), ("L0_xattn_bq", (0,)),
             ("L0_xattn_wkv", (1, 0)), ("L0_xattn_bkv", (0,)), ("L0_xattn_wp", (0, 1)), ("L0_xattn_bp", (0,)),
             ("L0_ffn_w_gate", (0, 1)), ("L0_ffn_wi_0", (0, 1, 2)), ("L0_ffn_wi_1", (0, 1, 2)),
             ("L0_ffn_wo", (0, 1, 2))]
    arrays, args = {}, []
    for name, axes in order:
        a = _np.ascontiguousarray(_np.transpose(_np.asarray(inputs[name]), axes))
        arrays[f"in_{name}_dram"] = a
        args.append(nc.dram_tensor(f"in_{name}_dram", a.shape, _mybir.dt.from_np(a.dtype), kind="ExternalInput").ap())
    args.append(nc.dram_tensor("out_0_dram", (B, N, C), F32, kind="ExternalOutput").ap())
    program(nc, *args)
    r = _run(nc, [arrays], core_ids=[0])
    return r.results[0]["out_0_dram"]
```

```python
from contextlib import ExitStack, contextmanager

import concourse.bass as bass
from concourse import mybir

F32 = mybir.dt.float32
F16 = mybir.dt.float16
BF16 = mybir.dt.bfloat16
I32 = mybir.dt.int32
U32 = mybir.dt.uint32
ALU = mybir.AluOpType
ACT = mybir.ActivationFunctionType
AX = mybir.AxisListType

P = 128
B, N, C = 8, 512, 512
M = 1601
H, DH = 16, 32
E, TOPK, FF = 8, 2, 256
CC = C // P
QT = N // P
HB = P // DH
NBLK = H // HB
KT = -(-M // P)
TAIL = M - (KT - 1) * P
VC = 2 * DH + 1
WSCALE = 64.0
EPS = 1e-5
ROUND = 12582912.0
QMAX = 127.0


@contextmanager
def phase(nc):
    with ExitStack() as held:
        sems = []

        def sem(name):
            sems.append(held.enter_context(nc.semaphore(name)))
            return sems[-1]

        with nc.Block() as block:
            yield block, sem
        for s in sems:
            nc.gpsimd.sem_clear(s)
        nc.all_engine_barrier()


class Steps:

    def __init__(self, eng, sem):
        self.eng, self.sem, self.n = eng, sem, 0

    def __call__(self, ins):
        self.n += 1
        ins.then_inc(self.sem, 1)
        self.eng.wait_ge(self.sem, self.n)


def sbuf(nc, held, name, shape, dt):
    return held.enter_context(nc.sbuf_tensor(name, shape, dt))


def banks(nc, held, names, dt=F32):
    n = 512 if dt == F32 else 1024
    return [held.enter_context(nc.psum_tensor(x, [P, n], dt)) for x in names]


def make_constants(nc, held):
    k = {
        "id32": sbuf(nc, held, "id32", [P, P], F32),
        "id16": sbuf(nc, held, "id16", [P, P], F16),
        "idb": sbuf(nc, held, "idb", [P, P], BF16),
        "ones": sbuf(nc, held, "ones", [P, P], F32),
    }
    with phase(nc) as (block, sem):
        filled, cut = sem("filled"), sem("cut")

        @block.gpsimd
        def _(pool):
            pool.memset(k["ones"][:, :], 1.0).then_inc(filled, 1)
            pool.wait_ge(filled, 1)
            pool.affine_select(out=k["id32"][:, :], in_=k["ones"][:, :], compare_op=ALU.is_equal, fill=0.0,
                               base=0, pattern=[[-1, P]], channel_multiplier=1).then_inc(cut, 1)

        @block.vector
        def _(dve):
            dve.wait_ge(cut, 1)
            dve.tensor_copy(k["id16"][:, :], k["id32"][:, :])
            dve.tensor_copy(k["idb"][:, :], k["id32"][:, :])
    return k


def quantize_weight(nc, k, tag, w, w_t, s_row):
    with ExitStack() as held, phase(nc) as (block, sem):
        w_n = sbuf(nc, held, tag + "w_n", [P, CC, C], F32)
        w_y = sbuf(nc, held, tag + "w_y", [P, CC, C], F32)
        w_q = sbuf(nc, held, tag + "w_q", [P, CC, C], BF16)
        amax = sbuf(nc, held, tag + "w_amax", [P, CC], F32)
        scale = sbuf(nc, held, tag + "w_scale", [P, CC], F32)
        inv = sbuf(nc, held, tag + "w_inv", [P, CC], F32)
        diag = sbuf(nc, held, tag + "w_diag", [P, CC, P], F32)
        ps_t = banks(nc, held, [tag + "ps_t0", tag + "ps_t1"], BF16)
        ps_s = banks(nc, held, [tag + "ps_s"])[0]
        loaded, step, quantized, spread, turned, rowed = (
            sem(x) for x in ("w_loaded", "w_step", "w_quantized", "w_spread", "w_turned", "w_rowed"))

        @block.sync
        def _(sp):
            sp.dma_start(w_n[:, :, :], w.rearrange("(t p) c -> p t c", p=P)).then_inc(loaded, 16)

        @block.vector
        def _(dve):
            done = Steps(dve, step)
            dve.wait_ge(loaded, 16)
            done(dve.tensor_reduce(amax[:, :], w_n[:, :, :], AX.X, ALU.max, apply_absolute_value=True))
            done(dve.tensor_scalar(scale[:, :], amax[:, :], 1.0 / QMAX, 1e-8, ALU.mult, ALU.max))
            done(dve.reciprocal(inv[:, :], scale[:, :]))
            for t in range(CC):
                dve.tensor_scalar(w_y[:, t, :], w_n[:, t, :], inv[:, t:t + 1], QMAX, ALU.mult, ALU.min)
                last = dve.tensor_scalar(diag[:, t, :], k["id32"][:, :], scale[:, t:t + 1], None, ALU.mult)
            last.then_inc(spread, 1)
            dve.wait_ge(spread, 1)
            done(dve.tensor_scalar(w_n[:, :, :], w_y[:, :, :], -QMAX, ROUND, ALU.max, ALU.add))
            dve.tensor_scalar(w_q[:, :, :], w_n[:, :, :], ROUND, None, ALU.subtract).then_inc(quantized, 1)
            for half in range(2):
                dve.wait_ge(turned, half + 1)
                dve.tensor_copy(w_t[:, 2 * half:2 * half + 2, :],
                                ps_t[half][:, :].rearrange("p (c o) -> p c o", c=2))
            dve.wait_ge(rowed, 1)
            dve.tensor_copy(s_row[:, :], ps_s[:, :])

        @block.tensor
        def _(pe):
            pe.wait_ge(spread, 1)
            for t in range(CC):
                last = pe.matmul(ps_s[:, t * P:(t + 1) * P], k["ones"][:, :], diag[:, t, :], start=True, stop=True)
            last.then_inc(rowed, 1)
            pe.wait_ge(quantized, 1)
            for half in range(2):
                for c in range(2 * half, 2 * half + 2):
                    for t in range(CC):
                        at = (c % 2) * C + t * P
                        last = pe.transpose(ps_t[half][:, at:at + P], w_q[:, t, c * P:(c + 1) * P], k["idb"][:, :])
                last.then_inc(turned, 1)


def split_kv_weight(nc, wkv_t, wkv):
    with ExitStack() as held, phase(nc) as (block, sem):
        raw = sbuf(nc, held, "kv_raw", [P, CC, 2 * C], F32)
        loaded, high = sem("kv_loaded"), sem("kv_high")

        @block.sync
        def _(sp):
            for c in range(CC):
                sp.dma_start(raw[:, c, :], wkv_t[c * P:(c + 1) * P, :]).then_inc(loaded, 16)

        @block.vector
        def _(dve):
            dve.wait_ge(loaded, 16 * CC)
            for c in range(CC):
                dve.tensor_scalar(wkv[:, 0, c, :], raw[:, c, :], WSCALE, None, ALU.mult).then_inc(high, 1)
            for c in range(CC):
                dve.wait_ge(high, c + 1)
                dve.scalar_tensor_tensor(out=wkv[:, 1, c, :], in0=raw[:, c, :], scalar=WSCALE,
                                         in1=wkv[:, 0, c, :], op0=ALU.mult, op1=ALU.subtract)


def inverse_std(dve, done, var, std, rstd, tmp):
    done(dve.reciprocal(rstd, std))
    done(dve.tensor_tensor(tmp, rstd, rstd, ALU.mult))
    done(dve.scalar_tensor_tensor(out=tmp, in0=var, scalar=EPS, in1=tmp, op0=ALU.add, op1=ALU.mult))
    done(dve.tensor_scalar(tmp, tmp, -0.5, 1.5, ALU.mult, ALU.add))
    done(dve.tensor_tensor(rstd, rstd, tmp, ALU.mult))


ROUNDS = 4


def project_queries(nc, k, x, wq_t, s_row, bq_row, q_nat, q_t):
    with ExitStack() as held:
        sb = lambda name, shape, dt=F32: sbuf(nc, held, "q_" + name, shape, dt)
        xt = [sb(f"xt{n}", [P, QT, C]) for n in range(2)]
        xm, xy = sb("xm", [P, QT, C]), sb("xy", [P, QT, C])
        xq = [sb(f"xq{n}", [P, QT, C], BF16) for n in range(2)]
        xqt = sb("xqt", [P, CC, N], BF16)
        q = [sb(f"q{n}", [P, QT, C]) for n in range(2)]
        q_hl = sb("hl", [P, 2, QT, C], F16)
        q_tt = [sb(f"tt{n}", [P, 2, NBLK, N], F16) for n in range(2)]
        st, mv = sb("st", [P, QT, 6]), sb("mv", [P, QT, 2])
        sx = [sb(f"sx{n}", [P, QT]) for n in range(2)]
        nmean, std, rstd, tmp, amax, inv, mul = (
            sb(n, [P, QT]) for n in ("nmean", "std", "rstd", "tmp", "amax", "inv", "mul"))
        ps_q = banks(nc, held, [f"q_ps{t}" for t in range(QT)])
        ps_x = banks(nc, held, ["q_px0", "q_px1"], BF16)
        ps_t = banks(nc, held, ["q_pt0", "q_pt1"], F16)
        with nc.Fori(0, B // ROUNDS) as i, phase(nc) as (block, sem):
            step, centred, rooted, quantized, turned, xqt_ready, projected, scaled = (
                sem("q_" + n) for n in ("step", "centred", "rooted", "quantized", "turned", "xqt_ready", "projected",
                                        "scaled"))
            q_ready, high, split, q_turned, tt_ready = (
                sem("q_" + n) for n in ("ready", "high", "split", "qturned", "tt_ready"))
            loaded, stored = ([sem(f"q_{x}{n}") for n in range(2)] for x in ("loaded", "stored"))

            def rows(a, n):
                return a[bass.ds(i * (ROUNDS * N) + n * N, N), :].rearrange("(t p) c -> p t c", p=P)

            @block.sync
            def _(sp):
                def load(n):
                    if n >= 2:
                        sp.wait_ge(rooted, 2 * (n - 1))
                    sp.dma_start(xt[n % 2][:, :, :], rows(x, n)).then_inc(loaded[n % 2], 16)

                load(0)
                load(1)
                for n in range(ROUNDS):
                    if n + 2 < ROUNDS:
                        load(n + 2)
                    sp.wait_ge(q_ready, n + 1)
                    sp.dma_start(rows(q_nat, n), q[n % 2][:, :, :]).then_inc(stored[n % 2], 16)
                    for part in range(2):
                        sp.wait_ge(tt_ready, 4 * n + 2 * part + 2)
                        sp.dma_start(q_t[part, :, :, bass.ds(i * (ROUNDS * N) + n * N, N)].rearrange("k p n -> p k n"),
                                     q_tt[n % 2][:, part, :, :]).then_inc(stored[n % 2], 16)
                for n in range(2):
                    sp.wait_ge(stored[n], 48 * ROUNDS // 2)

            @block.scalar
            def _(act):
                def centre(n):
                    act.wait_ge(centred, n + 1)
                    act.activation(std[:, :], mv[:, :, 1], ACT.Sqrt, bias=k["eps"][:, 0:1]).then_inc(rooted, 1)
                    for t in range(QT):
                        last = act.activation(xm[:, t, :], xt[n % 2][:, t, :], ACT.Identity, bias=nmean[:, t:t + 1])
                    last.then_inc(rooted, 1)

                def copy_integers(n):
                    for half in range(2):
                        act.wait_ge(turned, 2 * n + half + 1)
                        act.copy(xqt[:, 2 * half:2 * half + 2, :],
                                 ps_x[half][:, :].rearrange("p (c n) -> p c n", c=2)).then_inc(xqt_ready, 1)

                centre(0)
                copy_integers(0)
                centre(1)
                for n in range(ROUNDS):
                    if n + 1 < ROUNDS:
                        copy_integers(n + 1)
                    act.wait_ge(q_ready, n + 1)
                    act.copy(q_hl[:, 0, :, :], q[n % 2][:, :, :]).then_inc(high, 1)
                    if n + 2 < ROUNDS:
                        centre(n + 2)
                    for g in range(4):
                        act.wait_ge(q_turned, 4 * n + g + 1)
                        if n >= 2 and g == 0:
                            act.wait_ge(stored[n % 2], 48 * (n // 2))
                        act.copy(q_tt[n % 2][:, g // 2, 2 * (g % 2):2 * (g % 2) + 2, :],
                                 ps_t[g % 2][:, :].rearrange("p (c n) -> p c n", c=2)).then_inc(tt_ready, 1)

            @block.vector
            def _(dve):
                done = Steps(dve, step)

                def quantize(n):
                    dve.wait_ge(loaded[n % 2], 16 * (n // 2 + 1))
                    for t in range(QT):
                        last = dve.bn_stats(st[:, t, :], xt[n % 2][:, t, :])
                    done(last)
                    for t in range(QT):
                        last = dve.bn_aggr(mv[:, t, :], st[:, t, :])
                    done(last)
                    dve.tensor_scalar(nmean[:, :], mv[:, :, 0], -1.0, None, ALU.mult).then_inc(centred, 1)
                    dve.wait_ge(rooted, 2 * n + 1)
                    inverse_std(dve, done, mv[:, :, 1], std[:, :], rstd[:, :], tmp[:, :])
                    dve.wait_ge(rooted, 2 * n + 2)
                    done(dve.tensor_reduce(amax[:, :], xm[:, :, :], AX.X, ALU.max, apply_absolute_value=True))
                    done(dve.tensor_tensor(tmp[:, :], amax[:, :], rstd[:, :], ALU.mult))
                    done(dve.tensor_scalar(sx[n % 2][:, :], tmp[:, :], 1.0 / QMAX, 1e-8, ALU.mult, ALU.max))
                    done(dve.reciprocal(inv[:, :], sx[n % 2][:, :]))
                    done(dve.tensor_tensor(mul[:, :], inv[:, :], rstd[:, :], ALU.mult))
                    for t in range(QT):
                        last = dve.tensor_scalar(xy[:, t, :], xm[:, t, :], mul[:, t:t + 1], QMAX, ALU.mult, ALU.min)
                    done(last)
                    done(dve.tensor_scalar(xm[:, :, :], xy[:, :, :], -QMAX, ROUND, ALU.max, ALU.add))
                    if n >= 2:
                        dve.wait_ge(turned, 2 * (n - 1))
                    dve.tensor_scalar(xq[n % 2][:, :, :], xm[:, :, :], ROUND, None, ALU.subtract).then_inc(quantized, 1)

                quantize(0)
                for n in range(ROUNDS):
                    if n + 1 < ROUNDS:
                        quantize(n + 1)
                    if n >= 2:
                        dve.wait_ge(stored[n % 2], 48 * (n // 2))
                    for t in range(QT):
                        dve.wait_ge(projected, QT * n + t + 1)
                        dve.scalar_tensor_tensor(out=q[n % 2][:, t, :], in0=ps_q[t][:, :],
                                                 scalar=sx[n % 2][:, t:t + 1], in1=s_row[:, :], op0=ALU.mult,
                                                 op1=ALU.mult).then_inc(scaled, 1)

            @block.gpsimd
            def _(pool):
                for n in range(ROUNDS):
                    for t in range(QT):
                        pool.wait_ge(scaled, QT * n + t + 1)
                        last = pool.tensor_tensor(q[n % 2][:, t, :], q[n % 2][:, t, :], bq_row[:, :], ALU.add)
                    last.then_inc(q_ready, 1)
                    pool.wait_ge(high, n + 1)
                    pool.tensor_tensor(q_hl[:, 1, :, :], q[n % 2][:, :, :], q_hl[:, 0, :, :],
                                       ALU.subtract).then_inc(split, 1)

            @block.tensor
            def _(pe):
                def project(n):
                    pe.wait_ge(quantized, n + 1)
                    for half in range(2):
                        for c in range(2 * half, 2 * half + 2):
                            for t in range(QT):
                                at = (c % 2) * N + t * P
                                last = pe.transpose(ps_x[half][:, at:at + P], xq[n % 2][:, t, c * P:(c + 1) * P],
                                                    k["idb"][:, :])
                        last.then_inc(turned, 1)
                    pe.wait_ge(xqt_ready, 2 * (n + 1))
                    for t in range(QT):
                        if n >= 1:
                            pe.wait_ge(scaled, QT * (n - 1) + t + 1)
                        for c in range(CC):
                            last = pe.matmul(ps_q[t][:, :], xqt[:, c, t * P:(t + 1) * P], wq_t[:, c, :],
                                             start=(c == 0), stop=(c == CC - 1))
                        last.then_inc(projected, 1)

                project(0)
                for n in range(ROUNDS):
                    if n + 1 < ROUNDS:
                        project(n + 1)
                    for g in range(4):
                        if g == 0:
                            pe.wait_ge(high, n + 1)
                        if g == 2:
                            pe.wait_ge(split, n + 1)
                        if 4 * n + g >= 2:
                            pe.wait_ge(tt_ready, 4 * n + g - 1)
                        for kb in range(2 * (g % 2), 2 * (g % 2) + 2):
                            for t in range(QT):
                                at = (kb % 2) * N + t * P
                                last = pe.transpose(ps_t[g % 2][:, at:at + P], q_hl[:, g // 2, t, kb * P:(kb + 1) * P],
                                                    k["id16"][:, :])
                        last.then_inc(q_turned, 1)


TERMS = 3
GROUP = 2
GROUPS = -(-KT // GROUP)
SLOTS = HB * GROUPS
LAG = 3
NP = 4
KEY_CUTS = [0, 401, 801, 1201, M]
VALUE_TILES = [range(0, 4), range(4, 7), range(7, 10), range(10, KT)]
HALVES = [(0, 801), (801, M)]
SUM_LOW, SUM_HIGH = 0.5, float(2 ** 20)
OUT_HIGH = 1e30

TT = B * N // P
TILES = 72
assert TILES * P >= B * N * TOPK + E * (P - 1)
ZEROED = TILES // (B // 2 - 1)
assert ZEROED * (B // 2 - 1) == TILES and ZEROED % 4 == 0


def group_tiles(g):
    return range(GROUP * g, min(GROUP * g + GROUP, KT))


def rows_of(kt):
    return P if kt < KT - 1 else TAIL


def cost(job):
    kind, _, n = job
    return TERMS * CC * (KEY_CUTS[n + 1] - KEY_CUTS[n] if kind == "k" else C)


class Jobs:

    def __init__(self, units, attend, last):
        self.all = []
        self.slices = {}
        self.ends = {}
        self.keys_done = {}
        self.context_done = {}
        for v in units:
            new = [("k", v + 1, g) for g in range(4)] if v + 1 < 2 * NBLK or not last else []
            if v < 0:
                new += [("v", 0, t) for t in range(KT)]
            elif v < NBLK or not last:
                new += [("v", (v // NBLK + 1) % 2, t) for t in VALUE_TILES[v % NBLK]]
            at = max(v, 0) * SLOTS
            open_slots = SLOTS if any(job[0] == "v" for job in new) else 3 * GROUPS
            load = [len(group_tiles(s % GROUPS)) if s < open_slots else 0 for s in range(SLOTS)]
            slot_end = [sum(load[:s + 1]) * sum(map(cost, new)) / sum(load) for s in range(SLOTS)]
            spent = 0
            for n, job in enumerate(new):
                j = len(self.all)
                self.all.append(job)
                for m in range(TERMS * CC):
                    spent += cost(job) / (TERMS * CC)
                    s = at + (min(sum(e < spent - 0.5 for e in slot_end), SLOTS - 1) if attend else n)
                    self.slices.setdefault(s, []).append((j, m))
                self.ends.setdefault(s, []).append(j)
                if job[0] == "k":
                    self.keys_done[v + 1] = j + 1
            self.context_done[v] = len(self.all)
        self.slots = (max(units) + 1) * SLOTS if attend else len(self.all)


def attention_pass(nc, t, i, units, attend, last, loads):
    jobs = Jobs(units, attend, last)
    ends_by = {}
    with phase(nc) as (block, sem):
        scores, shifted, lows, used = (sem("a_" + x) for x in ("scores", "exp", "lows", "used"))
        projected, highs, job_done = (sem("a_" + x) for x in ("projected", "highs", "job_done"))
        keys_in, queries_in, ctx_in, out_stored = (
            [sem(f"a_{x}{n}") for n in range(2)] for x in ("keys_in", "queries_in", "ctx_in", "out_stored"))
        ctx_high, ctx_split = sem("a_ctx_high"), sem("a_ctx_split")
        out_copied, inverted, out_step, out_ready, checked, check_step = (
            sem("a_" + x) for x in ("out_copied", "inverted", "out_step", "out_ready", "checked", "check_step"))
        stacked = sorted(jobs.keys_done)

        def loads_of(v):
            return sum(1 for u in stacked if u % 2 == v % 2 and u <= v)

        piece = [(n, c, h) for n in range(len(loads)) for c in range(CC) for h in range(2)]

        def batch_of(v):
            return 2 * i + v // NBLK if v >= 0 else 0

        def slot_pieces(s):
            out = []
            for p, (n, c, h) in enumerate(piece):
                at = loads[n][0] * SLOTS + 3 * (c * 2 + h) if attend else 0
                if at == s:
                    out.append(p)
            return out

        def context_low(eng, p):
            n, c, h = piece[p]
            a, b = HALVES[h]
            eng.wait_ge(ctx_high, p + 1)
            eng.tensor_tensor(t["ctx"][loads[n][1]][:, 1, c, a:b], t["ctx_raw"][p % 2][:, 0:b - a],
                              t["ctx"][loads[n][1]][:, 0, c, a:b], ALU.subtract).then_inc(ctx_split, 1)

        @block.sync
        def _(sp):
            def load_queries(v):
                if attend and v - 2 >= 0:
                    sp.wait_ge(scores, SLOTS * (v - 1))
                for s in range(TERMS):
                    kb = v % NBLK
                    sp.dma_start(t["q_stack"][v % 2][s * DH:(s + 1) * DH, :, :],
                                 t["q_t"][1 if s == 2 else 0, kb, :, bass.ds(batch_of(v) * N, N)]
                                 .rearrange("(j d) n -> d j n", d=DH)).then_inc(queries_in[v % 2], 16)

            def stack_keys(v):
                sp.wait_ge(job_done, jobs.keys_done[v])
                for j in range(HB):
                    for s in range(TERMS):
                        sp.dma_start(t["k_stack"][v % 2][s * DH:(s + 1) * DH, j, :],
                                     t["k_parts"][j * DH:(j + 1) * DH, s % 2, :]).then_inc(keys_in[v % 2], 16)

            def load_context(n):
                v, par, batch = loads[n]
                for c in range(CC):
                    for h, (a, b) in enumerate(HALVES):
                        p = n * 2 * CC + 2 * c + h
                        if p >= 2:
                            sp.wait_ge(ctx_split, p - 1)
                        sp.dma_start(t["ctx_raw"][p % 2][:, 0:b - a],
                                     t["ctx_t"][bass.ds(batch, 1), c * P:(c + 1) * P, a:b]
                                     .rearrange("a p n -> p (a n)")).then_inc(ctx_in[p % 2], 16)

            def store_out(v):
                sp.wait_ge(out_ready, v + 1)
                sp.dma_start(t["o"][bass.ds(batch_of(v) * N, N), (v % NBLK) * P:(v % NBLK + 1) * P]
                             .rearrange("(t p) c -> p t c", p=P), t["o_tile"][v % 2][:, :, :]).then_inc(out_stored[v % 2], 16)

            def zero_rows(n):
                count = ZEROED // 4 * P
                sp.dma_start(t["xs"][bass.ds(i * (4 * count) + n * count, count), :]
                             .rearrange("(p r) (h c) -> p (r h) c", p=P, h=2),
                             t["zero"][:, None, :].to_broadcast([P, 2 * count // P, C])).then_inc(t["zeroed"], 16)

            for v in units:
                if attend and not last and v % NBLK < 2:
                    zero_rows(2 * (v // NBLK) + v % NBLK)
                if v + 1 < 2 * NBLK or not last:
                    load_queries(v + 1)
                for n in range(len(loads)):
                    if loads[n][0] == v:
                        load_context(n)
                if v + 1 in jobs.keys_done:
                    stack_keys(v + 1)
                if attend and v >= 1:
                    store_out(v - 1)
            if attend:
                store_out(units[-1])
                for n in range(2):
                    sp.wait_ge(out_stored[n], 16 * len(units) // 2)
            v = stacked[-1]
            sp.wait_ge(queries_in[v % 2], 16 * TERMS * loads_of(v))
            sp.wait_ge(keys_in[v % 2], 16 * TERMS * HB * loads_of(v))

        @block.tensor
        def _(pe):
            def do_scores(s):
                v, j, g = s // SLOTS, s % SLOTS // GROUPS, s % GROUPS
                if s >= 2:
                    pe.wait_ge(shifted, s - 1)
                if s % SLOTS == 0 and v > 0:
                    pe.wait_ge(keys_in[v % 2], 16 * TERMS * HB * loads_of(v))
                    pe.wait_ge(queries_in[v % 2], 16 * TERMS * loads_of(v))
                for n, kt in enumerate(group_tiles(g)):
                    r = rows_of(kt)
                    mm = pe.matmul(t["ps_s"][s % 2][0:r, n * N:(n + 1) * N],
                                   t["k_stack"][v % 2][0:TERMS * DH, j, kt * P:kt * P + r],
                                   t["q_stack"][v % 2][0:TERMS * DH, j, :], start=True, stop=True)
                mm.then_inc(scores, 1)

            def project(j, m):
                kind, where, n = jobs.all[j]
                if kind == "k":
                    par = where // NBLK % 2
                    c0, a, b = where % NBLK * P, KEY_CUTS[n], KEY_CUTS[n + 1]
                    rows, cols = P, b - a
                else:
                    par, rows, cols = where, rows_of(n), C
                if m == 0:
                    if j >= 2:
                        pe.wait_ge(job_done, j - 1)
                    for n_load, (v, p, _) in enumerate(loads):
                        if p == par and (not attend or j >= jobs.context_done[v]):
                            pe.wait_ge(ctx_split, 2 * CC * (n_load + 1))
                ps = t["ps_p"][j % 2][0:rows, 0:cols]
                c, term = m // TERMS, m % TERMS
                w_part, x_part = (0, 0, 1)[term], (0, 1, 0)[term]
                ctx = t["ctx"][par]
                if kind == "k":
                    lhs, rhs = t["wkv"][:, w_part, c, c0:c0 + P], ctx[:, x_part, c, a:b]
                else:
                    lhs, rhs = ctx[:, x_part, c, n * P:n * P + rows], t["wkv"][:, w_part, c, C:2 * C]
                mm = pe.matmul(ps, lhs, rhs, start=(m == 0), stop=(m == TERMS * CC - 1))
                if m == TERMS * CC - 1:
                    mm.then_inc(projected, 1)

            def do_values(s):
                v, j, g = s // SLOTS, s % SLOTS // GROUPS, s % GROUPS
                head = s // GROUPS
                pe.wait_ge(lows, s + 1)
                if g == 0 and head >= 2:
                    pe.wait_ge(out_copied, head - 1)
                p_high = t["p"][s % NP][:, :].bitcast(BF16).rearrange("p (n two) -> p n two", two=2)[:, :, 1]
                for n, kt in enumerate(group_tiles(g)):
                    r = rows_of(kt)
                    val = t["v"][v // NBLK % 2][0:r, kt, (v % NBLK) * HB + j, :]
                    for low, part in enumerate((p_high, t["p_low"][s % NP])):
                        for q in range(QT):
                            mm = pe.matmul(t["ps_o"][head % 2][:, q * VC:(q + 1) * VC],
                                           part[0:r, n * N + q * P:n * N + (q + 1) * P], val,
                                           start=(g == 0 and n == 0 and low == 0 and q == 0),
                                           stop=(kt == KT - 1 and low == 1), skip_group_check=True)
                mm.then_inc(used, 1)

            for s in range(jobs.slots):
                if attend:
                    do_scores(s)
                for j, m in jobs.slices.get(s, []):
                    project(j, m)
                if attend and s >= LAG:
                    do_values(s - LAG)
            if attend:
                for s in range(jobs.slots - LAG, jobs.slots):
                    do_values(s)

        @block.scalar
        def _(act):
            def exponentials(s):
                g = s % GROUPS
                tiles = group_tiles(g)
                r = rows_of(tiles[-1])
                act.wait_ge(scores, s + 1)
                if s >= NP:
                    act.wait_ge(used, s - NP + 1)
                act.activation(t["p"][s % NP][0:r, 0:len(tiles) * N], t["ps_s"][s % 2][0:r, 0:len(tiles) * N],
                               ACT.Exp, scale=float(DH) ** -0.5 / WSCALE).then_inc(shifted, 1)

            def job_high(j):
                kind, where, n = jobs.all[j]
                act.wait_ge(projected, j + 1)
                if kind == "k":
                    a, b = KEY_CUTS[n], KEY_CUTS[n + 1]
                    if n == 0 and loads_of(where - 1):
                        act.wait_ge(keys_in[(where - 1) % 2], 16 * TERMS * HB * loads_of(where - 1))
                    act.activation(t["k_parts"][:, 0, a:b], t["ps_p"][j % 2][:, 0:b - a], ACT.Identity,
                                   bias=t["bk"][:, where % NBLK:where % NBLK + 1]).then_inc(highs, 1)
                else:
                    r = rows_of(n)
                    if attend and j in first_value and where == 0:
                        act.wait_ge(used, NBLK * SLOTS)
                    act.copy(t["v"][where][0:r, n, :, 0:DH],
                             t["ps_p"][j % 2][0:r, :].rearrange("p (h d) -> p h d", d=DH)).then_inc(highs, 1)

            def copy_out(head):
                v, j = head // HB, head % HB
                act.wait_ge(used, GROUPS * (head + 1))
                if j == 0 and v >= 2:
                    act.wait_ge(out_ready, v - 1)
                act.copy(t["o_sums"][v % 2][:, j, :, :],
                         t["ps_o"][head % 2][:, 0:QT * VC].rearrange("p (q c) -> p q c", q=QT)).then_inc(out_copied, 1)

            def context_high(p):
                n, c, h = piece[p]
                a, b = HALVES[h]
                act.wait_ge(ctx_in[p % 2], 16 * (p // 2 + 1))
                if attend and (c, h) == (0, 0):
                    act.wait_ge(job_done, jobs.context_done[loads[n][0] - 1])
                act.copy(t["ctx"][loads[n][1]][:, 0, c, a:b], t["ctx_raw"][p % 2][:, 0:b - a]).then_inc(ctx_high, 1)

            first_value = {min([j for j, x in enumerate(jobs.all) if x[0] == "v" and x[1] == 0], default=-1)}
            if not attend:
                for p in range(2 * CC):
                    context_high(p)
            for s in range(jobs.slots):
                if attend:
                    exponentials(s)
                for j in jobs.ends.get(s - 1 if attend else s, []):
                    job_high(j)
                if not attend and 2 * CC + s < len(piece):
                    context_high(2 * CC + s)
                if attend:
                    for p in slot_pieces(s):
                        context_high(p)
                    if s > LAG and (s - LAG) % GROUPS == 0:
                        copy_out((s - LAG) // GROUPS - 1)
            if attend:
                for j in jobs.ends.get(jobs.slots - 1, []):
                    job_high(j)
                copy_out(jobs.slots // GROUPS - 1)

        @block.vector
        def _(dve):
            done = Steps(dve, check_step)

            def low_probabilities(s):
                g = s % GROUPS
                tiles = group_tiles(g)
                r, n = rows_of(tiles[-1]), len(tiles) * N
                dve.wait_ge(shifted, s + 1)
                full = t["p"][s % NP][0:r, 0:n]
                high = full.bitcast(BF16).rearrange("p (n two) -> p n two", two=2)[:, :, 1]
                dve.tensor_tensor(t["p_low"][s % NP][0:r, 0:n], full, high, ALU.subtract).then_inc(lows, 1)

            def job_low(j):
                kind, where, n = jobs.all[j]
                dve.wait_ge(highs, j + 1)
                if kind == "k":
                    a, b = KEY_CUTS[n], KEY_CUTS[n + 1]
                    dve.scalar_tensor_tensor(out=t["k_parts"][:, 1, a:b], in0=t["ps_p"][j % 2][:, 0:b - a],
                                             scalar=t["bk"][:, where % NBLK:where % NBLK + 1],
                                             in1=t["k_parts"][:, 0, a:b], op0=ALU.add,
                                             op1=ALU.subtract).then_inc(job_done, 1)
                else:
                    r = rows_of(n)
                    dve.tensor_tensor(t["v"][where][0:r, n, :, DH:2 * DH],
                                      t["ps_p"][j % 2][0:r, :].rearrange("p (h d) -> p h d", d=DH),
                                      t["v"][where][0:r, n, :, 0:DH], ALU.subtract).then_inc(job_done, 1)

            def invert(v):
                dve.wait_ge(out_copied, HB * (v + 1))
                if v >= 2:
                    dve.wait_ge(out_ready, v - 1)
                sums = t["o_sums"][v % 2][:, :, :, 2 * DH]
                dve.reciprocal(t["o_inv"][v % 2][:, :, :], sums).then_inc(inverted, 1)
                done(dve.scalar_tensor_tensor(out=t["fine"][:, :, :], in0=sums, scalar=SUM_LOW * WSCALE,
                                              in1=t["fine"][:, :, :], op0=ALU.is_ge, op1=ALU.mult))
                done(dve.scalar_tensor_tensor(out=t["fine"][:, :, :], in0=sums, scalar=SUM_HIGH * WSCALE,
                                              in1=t["fine"][:, :, :], op0=ALU.is_le, op1=ALU.mult))

            def check(v):
                dve.wait_ge(out_ready, v + 1)
                done(dve.tensor_reduce(t["o_total"][:, :], t["o_tile"][v % 2][:, :, :], AX.XY, ALU.add))
                done(dve.scalar_tensor_tensor(out=t["finite"][:, :], in0=t["o_total"][:, :], scalar=OUT_HIGH,
                                              in1=t["finite"][:, :], op0=ALU.is_le, op1=ALU.mult))
                dve.scalar_tensor_tensor(out=t["finite"][:, :], in0=t["o_total"][:, :], scalar=-OUT_HIGH,
                                         in1=t["finite"][:, :], op0=ALU.is_ge, op1=ALU.mult).then_inc(checked, 1)

            if not attend:
                for p in range(2 * CC):
                    context_low(dve, p)
            for s in range(jobs.slots):
                if attend:
                    low_probabilities(s)
                for j in jobs.ends.get(s - 1 if attend else s, []):
                    job_low(j)
                if not attend and 2 * CC + s < len(piece):
                    context_low(dve, 2 * CC + s)
                if attend and s > LAG + 2 and (s - LAG - 2) % SLOTS == 0:
                    invert((s - LAG - 2) // SLOTS - 1)
                if attend and s > LAG + 8 and (s - LAG - 8) % SLOTS == 0:
                    check((s - LAG - 8) // SLOTS - 1)
            if attend:
                for j in jobs.ends.get(jobs.slots - 1, []):
                    job_low(j)
                invert(units[-1])
                check(units[-1])

        @block.gpsimd
        def _(pool):
            out_done = Steps(pool, out_step)

            def normalise(v):
                sums, out = t["o_sums"][v % 2], t["o_tile"][v % 2]
                heads = out[:, :, :].rearrange("p q (j d) -> p j q d", d=DH)
                pool.wait_ge(out_copied, HB * (v + 1))
                if v >= 2:
                    pool.wait_ge(out_stored[v % 2], 16 * (v // 2))
                    pool.wait_ge(checked, v - 1)
                for j in range(HB):
                    last = pool.tensor_tensor(heads[:, j], sums[:, j, :, 0:DH], sums[:, j, :, DH:2 * DH], ALU.add)
                out_done(last)
                pool.wait_ge(inverted, v + 1)
                for j in range(HB):
                    last = pool.tensor_tensor(heads[:, j], heads[:, j],
                                              t["o_inv"][v % 2][:, j, :, None].to_broadcast([P, QT, DH]), ALU.mult)
                out_done(last)
                kb = v % NBLK
                pool.tensor_tensor(out[:, :, :], out[:, :, :],
                                   t["bv_row"][:, None, kb * P:(kb + 1) * P].to_broadcast([P, QT, P]),
                                   ALU.add).then_inc(out_ready, 1)

            for s in range(jobs.slots if attend else 0):
                for p in slot_pieces(s):
                    context_low(pool, p)
                if s > LAG + 2 and (s - LAG - 2) % SLOTS == 0:
                    normalise((s - LAG - 2) // SLOTS - 1)
            if attend:
                normalise(units[-1])


def attention(nc, t):
    with ExitStack() as held:
        sb = lambda name, shape, dt: sbuf(nc, held, name, shape, dt)
        t = dict(t)
        t["ctx"] = [sb(f"ctx{n}", [P, 2, CC, M], F16) for n in range(2)]
        t["v"] = [sb(f"v{n}", [P, KT, H, VC], F16) for n in range(2)]
        t["k_stack"] = [sb(f"k_stack{n}", [TERMS * DH, HB, M], F16) for n in range(2)]
        t["k_parts"] = sb("k_parts", [P, 2, M], F16)
        t["ctx_raw"] = [sb(f"ctx_raw{n}", [P, HALVES[0][1]], F32) for n in range(2)]
        t["p"] = [sb(f"p{n}", [P, GROUP * N], F32) for n in range(NP)]
        t["p_low"] = [sb(f"p_low{n}", [P, GROUP * N], F16) for n in range(NP)]
        t["q_stack"] = [sb(f"q_stack{n}", [TERMS * DH, HB, N], F16) for n in range(2)]
        t["o_sums"] = [sb(f"o_sums{n}", [P, HB, QT, VC], F32) for n in range(2)]
        t["o_inv"] = [sb(f"o_inv{n}", [P, HB, QT], F32) for n in range(2)]
        t["o_tile"] = [sb(f"o_tile{n}", [P, QT, P], F32) for n in range(2)]
        t["o_total"] = sb("o_total", [P, 1], F32)
        t["ps_s"] = [held.enter_context(nc.psum_tensor(f"ps_s{n}", [P, GROUP * N], F32)) for n in range(2)]
        t["ps_o"] = banks(nc, held, ["ps_o0", "ps_o1"])
        t["ps_p"] = banks(nc, held, ["ps_p0", "ps_p1"])
        with phase(nc) as (block, sem):
            @block.vector
            def _(dve):
                for n in range(2):
                    dve.memset(t["v"][n][:, :, :, 2 * DH], WSCALE)
                dve.memset(t["fine"][:, :, :], 1.0)
                dve.memset(t["finite"][:, :], 1.0)

        attention_pass(nc, t, 0, [-1], attend=False, last=False, loads=[(-1, 0, 0), (-1, 1, 1)])
        units = list(range(2 * NBLK))
        with nc.Fori(0, B // 2 - 1) as i:
            attention_pass(nc, t, i, units, attend=True, last=False,
                           loads=[(NBLK - 1, 0, 2 * i + 2), (2 * NBLK - 1, 1, 2 * i + 3)])
        attention_pass(nc, t, B // 2 - 1, units, attend=True, last=True, loads=[])


def judge_range(nc, k, t):
    with ExitStack() as held, phase(nc) as (block, sem):
        worst = sbuf(nc, held, "j_worst", [P, 1], F32)
        fit = sbuf(nc, held, "j_fit", [P, 1], F32)
        ps = banks(nc, held, ["j_ps"])[0]
        step, ready, summed = sem("j_step"), sem("j_ready"), sem("j_summed")

        @block.vector
        def _(dve):
            done = Steps(dve, step)
            done(dve.tensor_reduce(worst[:, :], t["fine"][:, :, :], AX.XY, ALU.min))
            dve.tensor_tensor(fit[:, :], worst[:, :], t["finite"][:, :], ALU.mult).then_inc(ready, 1)
            dve.wait_ge(summed, 1)
            dve.tensor_scalar(t["unfit"][:, :], ps[0:1, 0:1], float(P) - 0.5, None, ALU.is_lt)

        @block.tensor
        def _(pe):
            pe.wait_ge(ready, 1)
            pe.matmul(ps[0:1, 0:1], fit[:, :], k["ones"][:, 0:1], start=True, stop=True).then_inc(summed, 1)


def attention_with_maximum(nc, k, t):
    ROUNDS = [range(0, 8), range(8, KT)]
    with ExitStack() as held:
        sb = lambda name, shape: sbuf(nc, held, "g_" + name, shape, F32)
        ctx = sb("ctx", [P, CC, M])
        w = sb("w", [P, 2, CC, P])
        bk = sb("bk", [P, 1])
        bv = sb("bv", [P, P])
        q = sb("q", [P, QT, P])
        q_t = sb("q_t", [P, N])
        k_t = sb("k_t", [P, M])
        v = sb("v", [P, KT, P])
        prob = sb("prob", [P, M])
        prob_t = sb("prob_t", [P, KT, P])
        top, total, inv = sb("top", [P, 1]), sb("total", [P, 1]), sb("inv", [P, 1])
        out = sb("out", [P, QT, P])
        ps_s = held.enter_context(nc.psum_tensor("g_ps_s", [P, 2048], F32))
        ps_t = held.enter_context(nc.psum_tensor("g_ps_t", [P, 1024], F32))
        ps_p, ps_o = banks(nc, held, ["g_ps_p", "g_ps_o"])
        with nc.Fori(0, B) as b, nc.Fori(0, NBLK) as kb, phase(nc) as (block, sem):
            (loaded, q_turned, q_copied, projected, taken, scored, topped, raised, turned, copied, weighed, normed,
             biased, step, stored) = (
                sem("g_" + n) for n in
                ("loaded", "q_turned", "q_copied", "projected", "taken", "scored", "topped", "raised", "turned",
                 "copied", "weighed", "normed", "biased", "step", "stored"))
            STEPS = [(j, n) for j in range(HB) for n in range(QT)]
            scale = float(DH) ** -0.5

            @block.sync
            def _(sp):
                sp.dma_start(ctx[:, :, :], t["ctx_t"][bass.ds(b, 1), :, :].rearrange("a (c p) n -> p (a c) n", p=P)).then_inc(loaded, 16)
                for n in range(2):
                    sp.dma_start(w[:, n, :, :], t["wkv_t"][:, bass.ds(kb * P + n * C, P)].rearrange("(c p) f -> p c f", p=P)).then_inc(loaded, 16)
                with nc.allow_non_contiguous_dma(reason="one bias for each partition"):
                    sp.dma_start(bk[:, :], t["bkv"][bass.ds(kb * P, P)].rearrange("(p a) -> p a", a=1)).then_inc(loaded, 16)
                sp.dma_start(bv[:, :], t["bkv"][bass.ds(kb * P + C, P)][None, :].to_broadcast([P, P])).then_inc(loaded, 16)
                sp.dma_start(q[:, :, :], t["q_nat"][bass.ds(b * N, N), bass.ds(kb * P, P)].rearrange("(t p) c -> p t c", p=P)).then_inc(loaded, 16)
                sp.wait_ge(biased, 1)
                sp.dma_start(t["o"][bass.ds(b * N, N), bass.ds(kb * P, P)].rearrange("(t p) c -> p t c", p=P), out[:, :, :]).then_inc(stored, 16)
                sp.wait_ge(stored, 16)

            @block.tensor
            def _(pe):
                pe.wait_ge(loaded, 96)
                for n in range(QT):
                    last = pe.transpose(ps_o[:, n * P:(n + 1) * P], q[:, n, :], k["id32"][:, :])
                last.then_inc(q_turned, 1)
                for n in range(4):
                    a, e = KEY_CUTS[n], KEY_CUTS[n + 1]
                    if n > 0:
                        pe.wait_ge(taken, n)
                    for c in range(CC):
                        last = pe.matmul(ps_p[:, 0:e - a], w[:, 0, c, :], ctx[:, c, a:e], start=(c == 0), stop=(c == CC - 1))
                    last.then_inc(projected, 1)
                for n in range(KT):
                    r = rows_of(n)
                    pe.wait_ge(taken, n + 4)
                    for c in range(CC):
                        last = pe.matmul(ps_p[0:r, 0:P], ctx[:, c, n * P:n * P + r], w[:, 1, c, :], start=(c == 0), stop=(c == CC - 1))
                    last.then_inc(projected, 1)
                pe.wait_ge(taken, KT + 4)
                pe.wait_ge(q_copied, 1)
                for i, (j, n) in enumerate(STEPS):
                    if i > 0:
                        pe.wait_ge(raised, i)
                    for a in range(0, M, 512):
                        e = min(a + 512, M)
                        last = pe.matmul(ps_s[:, a:e], q_t[j * DH:(j + 1) * DH, n * P:(n + 1) * P],
                                         k_t[j * DH:(j + 1) * DH, a:e], start=True, stop=True)
                    last.then_inc(scored, 1)
                    pe.wait_ge(raised, i + 1)
                    for m, tiles in enumerate(ROUNDS):
                        if i > 0 or m > 0:
                            pe.wait_ge(copied, 2 * i + m)
                        for x, kt in enumerate(tiles):
                            r = rows_of(kt)
                            last = pe.transpose(ps_t[0:r, x * P:(x + 1) * P], prob[:, kt * P:kt * P + r], k["id32"][:, :])
                        last.then_inc(turned, 1)
                    pe.wait_ge(copied, 2 * i + 2)
                    if i > 0:
                        pe.wait_ge(normed, i)
                    for kt in range(KT):
                        r = rows_of(kt)
                        last = pe.matmul(ps_o[:, 0:DH], prob_t[0:r, kt, :], v[0:r, kt, j * DH:(j + 1) * DH],
                                         start=(kt == 0), stop=(kt == KT - 1))
                    last.then_inc(weighed, 1)

            @block.scalar
            def _(act):
                for i in range(len(STEPS)):
                    act.wait_ge(topped, i + 1)
                    if i > 0:
                        act.wait_ge(turned, 2 * i)
                        act.wait_ge(normed, i)
                    act.activation(prob[:, :], ps_s[:, 0:M], ACT.Exp, bias=top[:, 0:1], scale=scale,
                                   accum_out=total[:, 0:1]).then_inc(raised, 1)

            @block.vector
            def _(dve):
                done = Steps(dve, step)
                dve.wait_ge(q_turned, 1)
                dve.tensor_copy(q_t[:, :], ps_o[:, :]).then_inc(q_copied, 1)
                for n in range(4):
                    a, e = KEY_CUTS[n], KEY_CUTS[n + 1]
                    dve.wait_ge(projected, n + 1)
                    dve.tensor_scalar(k_t[:, a:e], ps_p[:, 0:e - a], bk[:, 0:1], None, ALU.add).then_inc(taken, 1)
                for n in range(KT):
                    r = rows_of(n)
                    dve.wait_ge(projected, n + 5)
                    dve.tensor_copy(v[0:r, n, :], ps_p[0:r, 0:P]).then_inc(taken, 1)
                for i, (j, n) in enumerate(STEPS):
                    dve.wait_ge(scored, i + 1)
                    if i > 0:
                        dve.wait_ge(raised, i)
                    done(dve.tensor_reduce(top[:, :], ps_s[:, 0:M], AX.X, ALU.max))
                    dve.tensor_scalar(top[:, :], top[:, :], -scale, None, ALU.mult).then_inc(topped, 1)
                    for m, tiles in enumerate(ROUNDS):
                        dve.wait_ge(turned, 2 * i + m + 1)
                        if m == 0 and i > 0:
                            dve.wait_ge(weighed, i)
                        whole = [kt for kt in tiles if rows_of(kt) == P]
                        cols = len(whole) * P
                        last = dve.tensor_copy(prob_t[:, whole[0]:whole[-1] + 1, :],
                                               ps_t[:, 0:cols].rearrange("p (n q) -> p n q", q=P))
                        if len(whole) < len(tiles):
                            last = dve.tensor_copy(prob_t[0:TAIL, KT - 1, :], ps_t[0:TAIL, cols:cols + P])
                        last.then_inc(copied, 1)
                    dve.wait_ge(raised, i + 1)
                    done(dve.reciprocal(inv[:, :], total[:, :]))
                    dve.wait_ge(weighed, i + 1)
                    dve.tensor_scalar(out[:, n, j * DH:(j + 1) * DH], ps_o[:, 0:DH], inv[:, 0:1], None,
                                      ALU.mult).then_inc(normed, 1)
                dve.wait_ge(normed, len(STEPS))
                dve.tensor_tensor(out[:, :, :], out[:, :, :], bv[:, None, :].to_broadcast([P, QT, P]),
                                  ALU.add).then_inc(biased, 1)


def project_outputs(nc, k, t):
    with ExitStack() as held:
        sb = lambda name, shape, dt=F32: sbuf(nc, held, "u_" + name, shape, dt)
        o, xin, x2 = ([sb(f"{x}{n}", [P, QT, C]) for n in range(2)] for x in ("o", "xin", "x2"))
        oy, y, xn = sb("oy", [P, QT, C]), sb("y", [P, QT, C]), sb("xn", [P, QT, C])
        oq = [sb(f"oq{n}", [P, QT, C], BF16) for n in range(2)]
        oqt = sb("oqt", [P, CC, N], BF16)
        parts = [sb(f"parts{n}", [P, QT, 2, C], F16) for n in range(2)]
        parts_t = sb("parts_t", [P, 2, CC, N], F16)
        pair = sb("pair", [P, QT, 2 * E])
        st, mv = sb("st", [P, QT, 6]), sb("mv", [P, QT, 2])
        so = [sb(f"so{n}", [P, QT]) for n in range(2)]
        amax, inv, std, rstd, tmp, shift = (sb(n, [P, QT]) for n in ("amax", "inv", "std", "rstd", "tmp", "shift"))
        ps_y = banks(nc, held, [f"u_py{n}" for n in range(QT)])
        ps_b = banks(nc, held, ["u_pb0", "u_pb1"], BF16)
        ps_t = [b[:, :].bitcast(F16) for b in ps_b]
        ps_g = banks(nc, held, ["u_pg"])[0]
        with nc.Fori(0, B // ROUNDS) as i, phase(nc) as (block, sem):
            (step, quantized, turned, copied, projected, biased, scaled, x2_ready, measured, rooted, shifted,
             normed, high, split, xn_turned, xn_copied, gated, logits_in) = (
                sem("u_" + n) for n in
                ("step", "quantized", "turned", "copied", "projected", "biased", "scaled", "x2_ready", "measured",
                 "rooted", "shifted", "normed", "high", "split", "xn_turned", "xn_copied", "gated", "logits_in"))
            o_in, x_in, x2_out, xn_out = (
                [sem(f"u_{x}{n}") for n in range(2)] for x in ("o_in", "x_in", "x2_out", "xn_out"))

            @block.sync
            def _(sp):
                rows = lambda a, n: a[bass.ds(i * (ROUNDS * N) + n * N, N), :].rearrange("(t p) c -> p t c", p=P)

                def load(n):
                    if n >= 2:
                        sp.wait_ge(quantized, n - 1)
                        sp.wait_ge(x2_ready, QT * (n - 1))
                    sp.dma_start(o[n % 2][:, :, :], rows(t["o"], n)).then_inc(o_in[n % 2], 16)
                    sp.dma_start(xin[n % 2][:, :, :], rows(t["x"], n)).then_inc(x_in[n % 2], 16)

                load(0)
                load(1)
                for n in range(ROUNDS):
                    sp.wait_ge(x2_ready, QT * (n + 1))
                    sp.dma_start(rows(t["x2"], n), x2[n % 2][:, :, :]).then_inc(x2_out[n % 2], 16)
                    if n + 2 < ROUNDS:
                        load(n + 2)
                    sp.wait_ge(split, n + 1)
                    sp.dma_start(t["xn"][:, bass.ds(i * (ROUNDS * QT) + n * QT, QT), :],
                                 parts[n % 2][:, :, :, :].rearrange("p t s c -> p t (s c)")).then_inc(xn_out[n % 2], 16)
                for n in range(2):
                    sp.wait_ge(x2_out[n], 16 * ROUNDS // 2)
                    sp.wait_ge(xn_out[n], 16 * ROUNDS // 2)

            @block.gpsimd
            def _(pool):
                def add_bias(n):
                    pool.wait_ge(x_in[n % 2], 16 * (n // 2 + 1))
                    pool.tensor_tensor(xin[n % 2][:, :, :], xin[n % 2][:, :, :],
                                       t["bp_row"][:, None, :].to_broadcast([P, QT, C]), ALU.add).then_inc(biased, 1)

                add_bias(0)
                for n in range(ROUNDS):
                    pool.wait_ge(biased, n + 1)
                    if n >= 2:
                        pool.wait_ge(x2_out[n % 2], 16 * (n // 2))
                        pool.wait_ge(normed, n - 1)
                    for m in range(QT):
                        pool.wait_ge(scaled, QT * n + m + 1)
                        pool.tensor_tensor(x2[n % 2][:, m, :], y[:, m, :], xin[n % 2][:, m, :],
                                           ALU.add).then_inc(x2_ready, 1)
                    if n + 1 < ROUNDS:
                        add_bias(n + 1)
                    pool.wait_ge(high, n + 1)
                    pool.tensor_tensor(parts[n % 2][:, :, 1, :], xn[:, :, :], parts[n % 2][:, :, 0, :],
                                       ALU.subtract).then_inc(split, 1)

            @block.scalar
            def _(act):
                def copy_integers(n):
                    for half in range(2):
                        act.wait_ge(turned, 2 * n + half + 1)
                        act.copy(oqt[:, 2 * half:2 * half + 2, :],
                                 ps_b[half][:, :].rearrange("p (c n) -> p c n", c=2)).then_inc(copied, 1)

                copy_integers(0)
                for n in range(ROUNDS):
                    if n + 1 < ROUNDS:
                        copy_integers(n + 1)
                    act.wait_ge(measured, n + 1)
                    act.activation(std[:, :], mv[:, :, 1], ACT.Sqrt, bias=k["eps"][:, 0:1]).then_inc(rooted, 1)
                    act.wait_ge(shifted, n + 1)
                    if n >= 1:
                        act.wait_ge(split, n)
                    for m in range(QT):
                        last = act.activation(xn[:, m, :], x2[n % 2][:, m, :], ACT.Identity, bias=shift[:, m:m + 1],
                                              scale=rstd[:, m:m + 1])
                    last.then_inc(normed, 1)
                    act.wait_ge(normed, n + 1)
                    if n >= 2:
                        act.wait_ge(xn_out[n % 2], 16 * (n // 2))
                    act.copy(parts[n % 2][:, :, 0, :], xn[:, :, :]).then_inc(high, 1)
                    for g in range(4):
                        act.wait_ge(xn_turned, 4 * n + g + 1)
                        if n >= 1 and g == 0:
                            act.wait_ge(gated, n)
                        act.copy(parts_t[:, g // 2, 2 * (g % 2):2 * (g % 2) + 2, :],
                                 ps_t[g % 2].rearrange("p (c n) -> p c n", c=2)).then_inc(xn_copied, 1)

            @block.vector
            def _(dve):
                done = Steps(dve, step)

                def quantize(n):
                    dve.wait_ge(o_in[n % 2], 16 * (n // 2 + 1))
                    done(dve.tensor_reduce(amax[:, :], o[n % 2][:, :, :], AX.X, ALU.max, apply_absolute_value=True))
                    done(dve.tensor_scalar(so[n % 2][:, :], amax[:, :], 1.0 / QMAX, 1e-8, ALU.mult, ALU.max))
                    done(dve.reciprocal(inv[:, :], so[n % 2][:, :]))
                    for m in range(QT):
                        last = dve.tensor_scalar(oy[:, m, :], o[n % 2][:, m, :], inv[:, m:m + 1], QMAX, ALU.mult, ALU.min)
                    done(last)
                    done(dve.tensor_scalar(o[n % 2][:, :, :], oy[:, :, :], -QMAX, ROUND, ALU.max, ALU.add))
                    if n >= 2:
                        dve.wait_ge(turned, 2 * (n - 1))
                    dve.tensor_scalar(oq[n % 2][:, :, :], o[n % 2][:, :, :], ROUND, None, ALU.subtract).then_inc(quantized, 1)

                def read_logits(n):
                    dve.wait_ge(gated, n + 1)
                    dve.tensor_copy(pair[:, :, :],
                                    ps_g[:, 0:QT * 2 * E].rearrange("p (t e) -> p t e", t=QT)).then_inc(logits_in, 1)
                    dve.wait_ge(logits_in, n + 1)
                    done(dve.tensor_tensor(t["logits"][:, bass.ds(i * (ROUNDS * QT) + n * QT, QT), :], pair[:, :, 0:E],
                                           pair[:, :, E:2 * E], ALU.add))

                quantize(0)
                for n in range(ROUNDS):
                    if n + 1 < ROUNDS:
                        quantize(n + 1)
                    for m in range(QT):
                        dve.wait_ge(projected, QT * n + m + 1)
                        if n >= 1 and m == 0:
                            dve.wait_ge(x2_ready, QT * n)
                        dve.scalar_tensor_tensor(out=y[:, m, :], in0=ps_y[m][:, :], scalar=so[n % 2][:, m:m + 1],
                                                 in1=t["sp_row"][:, :], op0=ALU.mult, op1=ALU.mult).then_inc(scaled, 1)
                    if n >= 1:
                        read_logits(n - 1)
                        dve.wait_ge(normed, n)
                    for m in range(QT):
                        dve.wait_ge(x2_ready, QT * n + m + 1)
                        last = dve.bn_stats(st[:, m, :], x2[n % 2][:, m, :])
                    done(last)
                    for m in range(QT):
                        last = dve.bn_aggr(mv[:, m, :], st[:, m, :])
                    last.then_inc(measured, 1)
                    dve.wait_ge(rooted, n + 1)
                    inverse_std(dve, done, mv[:, :, 1], std[:, :], rstd[:, :], tmp[:, :])
                    dve.scalar_tensor_tensor(out=shift[:, :], in0=mv[:, :, 0], scalar=-1.0, in1=rstd[:, :],
                                             op0=ALU.mult, op1=ALU.mult).then_inc(shifted, 1)
                read_logits(ROUNDS - 1)

            @block.tensor
            def _(pe):
                def project(n):
                    pe.wait_ge(quantized, n + 1)
                    if n >= 2:
                        pe.wait_ge(xn_copied, 4 * (n - 1))
                    for half in range(2):
                        for c in range(2 * half, 2 * half + 2):
                            for m in range(QT):
                                at = (c % 2) * N + m * P
                                last = pe.transpose(ps_b[half][:, at:at + P], oq[n % 2][:, m, c * P:(c + 1) * P],
                                                    k["idb"][:, :])
                        last.then_inc(turned, 1)
                    pe.wait_ge(copied, 2 * (n + 1))
                    for m in range(QT):
                        if n >= 1:
                            pe.wait_ge(scaled, QT * (n - 1) + m + 1)
                        for c in range(CC):
                            last = pe.matmul(ps_y[m][:, :], oqt[:, c, m * P:(m + 1) * P], t["wp_t"][:, c, :],
                                             start=(c == 0), stop=(c == CC - 1))
                        last.then_inc(projected, 1)

                project(0)
                for n in range(ROUNDS):
                    if n + 1 < ROUNDS:
                        project(n + 1)
                    for g in range(4):
                        if g == 0:
                            pe.wait_ge(high, n + 1)
                        if g == 2:
                            pe.wait_ge(split, n + 1)
                        if g >= 2:
                            pe.wait_ge(xn_copied, 4 * n + g - 1)
                        for c in range(2 * (g % 2), 2 * (g % 2) + 2):
                            for m in range(QT):
                                at = (c % 2) * N + m * P
                                last = pe.transpose(ps_t[g % 2][:, at:at + P],
                                                    parts[n % 2][:, m, g // 2, c * P:(c + 1) * P], k["id16"][:, :])
                        last.then_inc(xn_turned, 1)
                    pe.wait_ge(xn_copied, 4 * (n + 1))
                    if n >= 1:
                        pe.wait_ge(logits_in, n)
                    for m in range(QT):
                        for part in range(2):
                            for c in range(CC):
                                last = pe.matmul(ps_g[:, m * 2 * E:(m + 1) * 2 * E],
                                                 parts_t[:, part, c, m * P:(m + 1) * P], t["gate"][:, c, :],
                                                 start=(part == 0 and c == 0), stop=(part == 1 and c == CC - 1))
                    last.then_inc(gated, 1)


PIECES = 3
MB = FF // P


def route(nc, k, t):
    with ExitStack() as held, phase(nc) as (block, sem):
        raw = [sbuf(nc, held, f"e_raw{n}", [P, 2, 2 * FF], F32) for n in range(PIECES)]
        loaded = [sem(f"e_loaded{n}") for n in range(PIECES)]
        high, split = sem("e_high"), sem("e_split")

        def weight_piece(e, n, part):
            return t["wi"][:, e, part, 2 * n:2 * n + 2, :] if n < 2 else t["wo"][:, e, part, :, :]

        sb = lambda name, shape, dt=F32: sbuf(nc, held, "r_" + name, shape, dt)
        best = sb("best", [P, TT, 8])
        index = sb("index", [P, TT, 8], U32)
        chosen = sb("chosen", [P, TOPK, TT])
        hot = sb("hot", [P, TOPK, TT, E])
        any_hot = sb("any_hot", [P, TT, E])
        any_hot_b = sb("any_hot_b", [P, TT, E], BF16)
        total, sum_a, sum_b, place = (sb(n, [P, TT, E]) for n in ("total", "sum_a", "sum_b", "place"))
        picked = sb("picked", [P, TOPK, TT, E])
        tiles, ends, ends_b, starts, base = (sb(n, [P, E]) for n in ("tiles", "ends", "ends_b", "starts", "base"))
        gap, ratio, first = (sb(n, [P, TT]) for n in ("gap", "ratio", "first"))
        pos = sb("pos", [P, TOPK, TT])
        experts_i = sb("experts_i", [P, E], I32)
        experts = sb("experts", [P, E])
        tile_i = sb("tile_i", [1, TILES], I32)
        tile_f = sb("tile_f", [1, TILES])
        passed = sb("passed", [1, TILES, E])
        of_tile = sb("of_tile", [1, TILES])
        before = sb("before", [P, P])
        before_b = sb("before_b", [P, P], BF16)
        ones_b = sb("ones_b", [P, P], BF16)
        ps_before, ps_total = banks(nc, held, ["r_pb", "r_pt"])
        made, step, hot_ready, summed, gap_ready, ratio_ready, routed = (
            sem("r_" + n) for n in ("made", "step", "hot_ready", "summed", "gap_ready", "ratio_ready", "routed"))
        stored, fetched = sem("r_stored"), sem("r_fetched")

        @block.gpsimd
        def _(pool):
            pool.iota(experts_i[:, :], [[1, E]], base=0, channel_multiplier=0)
            pool.iota(tile_i[:, :], [[1, TILES]], base=0, channel_multiplier=0)
            pool.affine_select(out=before[:, :], in_=k["ones"][:, :], compare_op=ALU.is_gt, fill=0.0, base=0,
                               pattern=[[1, P]], channel_multiplier=-1).then_inc(made, 1)
            for n in range(TT):
                for c in range(TOPK):
                    if n == 0 and c == 0:
                        pool.wait_ge(routed, 1)
                        pool.wait_ge(t["zeroed"], 64 * (B // 2 - 1))
                    pool.indirect_dma_start(
                        out=t["xs"][:, :], out_offset=bass.IndirectOffsetOnAxis(ap=t["rows"][:, c, n:n + 1], axis=0),
                        in_=t["xn"][:, n, :], in_offset=None).then_inc(stored, 16)
            pool.wait_ge(stored, 16 * TT * TOPK)

        @block.sync
        def _(sp):
            for e in range(E):
                for n in range(PIECES):
                    if e >= 1:
                        sp.wait_ge(split, PIECES * (e - 1) + n + 1)
                    for h in range(2):
                        if n < 2:
                            sp.dma_start(raw[n][:, :, h * FF:(h + 1) * FF],
                                         (t["wi_0"], t["wi_1"])[h][e, n * 2 * P:(n + 1) * 2 * P, :]
                                         .rearrange("(c p) f -> p c f", p=P)).then_inc(loaded[n], 16)
                        else:
                            sp.dma_start(raw[n][:, h, :], t["w_out"][e, h * P:(h + 1) * P, :]).then_inc(loaded[n], 16)

        @block.scalar
        def _(act):
            act.wait_ge(gap_ready, 1)
            act.activation(ratio[:, :], gap[:, :], ACT.Exp, scale=1.0 / WSCALE).then_inc(ratio_ready, 1)
            for e in range(E):
                for n in range(PIECES):
                    act.wait_ge(loaded[n], 32 * (e + 1))
                    act.mul(weight_piece(e, n, 0), raw[n][:, :, :], WSCALE).then_inc(high, 1)

        @block.tensor
        def _(pe):
            pe.wait_ge(hot_ready, 1)
            flat = any_hot_b[:, :, :].rearrange("p t e -> p (t e)")
            pe.matmul(ps_before[:, 0:TT * E], before_b[:, :], flat, start=True, stop=True)
            pe.matmul(ps_total[:, 0:TT * E], ones_b[:, :], flat, start=True, stop=True).then_inc(summed, 1)

        @block.vector
        def _(dve):
            done = Steps(dve, step)
            for n in range(TT):
                last = dve.max(best[:, n, :], t["logits"][:, n, :])
            done(last)
            for n in range(TT):
                last = dve.max_index(index[:, n, :], best[:, n, :], t["logits"][:, n, :])
            done(last)
            dve.tensor_tensor(gap[:, :], best[:, :, 1], best[:, :, 0], ALU.subtract).then_inc(gap_ready, 1)
            dve.wait_ge(made, 1)
            dve.tensor_copy(experts[:, :], experts_i[:, :])
            dve.tensor_copy(before_b[:, :], before[:, :])
            dve.memset(ones_b[:, :], 1.0)
            dve.tensor_copy(tile_f[:, :], tile_i[:, :])
            done(dve.tensor_copy(chosen[:, :, :], index[:, :, 0:TOPK].rearrange("p t c -> p c t")))
            for c in range(TOPK):
                last = dve.tensor_tensor(hot[:, c, :, :], experts[:, None, :].to_broadcast([P, TT, E]),
                                         chosen[:, c, :, None].to_broadcast([P, TT, E]), ALU.is_equal)
            done(last)
            done(dve.tensor_tensor(any_hot[:, :, :], hot[:, 0, :, :], hot[:, 1, :, :], ALU.add))
            dve.tensor_copy(any_hot_b[:, :, :], any_hot[:, :, :]).then_inc(hot_ready, 1)
            dve.wait_ge(summed, 1)
            flat = lambda a: a[:, :, :].rearrange("p t e -> p (t e)")
            dve.tensor_copy(flat(total), ps_total[:, 0:TT * E])
            done(dve.tensor_copy(flat(sum_a), ps_total[:, 0:TT * E]))
            src, dst = sum_a, sum_b
            for by in (1, 2, 4, 8, 16):
                dve.tensor_copy(dst[:, 0:by, :], src[:, 0:by, :])
                done(dve.tensor_tensor(dst[:, by:, :], src[:, by:, :], src[:, 0:TT - by, :], ALU.add))
                src, dst = dst, src
            done(dve.tensor_scalar(tiles[:, :], src[:, TT - 1, :], float(P - 1), 1.0 / P, ALU.add, ALU.mult))
            done(dve.tensor_scalar(tiles[:, :], tiles[:, :], -0.5 + 0.25 / P, ROUND, ALU.add, ALU.add))
            done(dve.tensor_scalar(tiles[:, :], tiles[:, :], ROUND, None, ALU.subtract))
            done(dve.tensor_copy(ends[:, :], tiles[:, :]))
            e_src, e_dst = ends, ends_b
            for by in (1, 2, 4):
                dve.tensor_copy(e_dst[:, 0:by], e_src[:, 0:by])
                done(dve.tensor_tensor(e_dst[:, by:], e_src[:, by:], e_src[:, 0:E - by], ALU.add))
                e_src, e_dst = e_dst, e_src
            done(dve.tensor_tensor(starts[:, :], e_src[:, :], tiles[:, :], ALU.subtract))
            done(dve.tensor_scalar(base[:, :], starts[:, :], float(P), None, ALU.mult))
            done(dve.tensor_tensor(place[:, :, :], src[:, :, :], total[:, :, :], ALU.subtract))
            done(dve.tensor_tensor(place[:, :, :], place[:, :, :], base[:, None, :].to_broadcast([P, TT, E]), ALU.add))
            done(dve.tensor_tensor(flat(place), flat(place), ps_before[:, 0:TT * E], ALU.add))
            for c in range(TOPK):
                last = dve.tensor_tensor(picked[:, c, :, :], hot[:, c, :, :], place[:, :, :], ALU.mult)
            done(last)
            done(dve.tensor_reduce(pos[:, :, :], picked[:, :, :, :], AX.X, ALU.add))
            dve.tensor_copy(t["rows"][:, :, :], pos[:, :, :]).then_inc(routed, 1)
            done(dve.tensor_tensor(passed[:, :, :], tile_f[:, :, None].to_broadcast([1, TILES, E]),
                                   starts[0:1, None, :].to_broadcast([1, TILES, E]), ALU.is_ge))
            done(dve.tensor_reduce(of_tile[:, :], passed[:, :, :], AX.X, ALU.add))
            done(dve.tensor_scalar(of_tile[:, :], of_tile[:, :], -1.0, None, ALU.add))
            dve.tensor_copy(t["expert_of"][:, :], of_tile[:, :])
            dve.wait_ge(ratio_ready, 1)
            done(dve.tensor_scalar(first[:, :], ratio[:, :], 1.0, None, ALU.add))
            done(dve.reciprocal(first[:, :], first[:, :]))
            dve.tensor_scalar(t["weights"][:, 0, :], first[:, :], 1.0 / WSCALE, None, ALU.mult)
            dve.scalar_tensor_tensor(out=t["weights"][:, 1, :], in0=ratio[:, :], scalar=1.0 / WSCALE,
                                     in1=first[:, :], op0=ALU.mult, op1=ALU.mult)
            for e in range(E):
                for n in range(PIECES):
                    dve.wait_ge(high, PIECES * e + n + 1)
                    flat = lambda a: a.rearrange("p a b -> p (a b)")
                    dve.scalar_tensor_tensor(out=flat(weight_piece(e, n, 1)), in0=flat(raw[n][:, :, :]),
                                             scalar=WSCALE, in1=flat(weight_piece(e, n, 0)), op0=ALU.mult,
                                             op1=ALU.subtract).then_inc(split, 1)


RUN = 18
BACK = TT * RUN // TILES
assert BACK * TILES == TT * RUN and 2 * BACK <= RUN + 3


def run_experts(nc, k, t):
    with ExitStack() as held:
        sb = lambda name, shape, dt: sbuf(nc, held, "f_" + name, shape, dt)
        xs = [sb(f"xs{n}", [P, 2 * C], F16) for n in range(3)]
        xt = [sb(f"xt{n}", [P, 2, CC, P], F16) for n in range(2)]
        gate = [sb(f"gate{n}", [P, FF], F32) for n in range(2)]
        inner = [sb(f"inner{n}", [P, FF], F32) for n in range(2)]
        parts = [sb(f"parts{n}", [P, 2, FF], F16) for n in range(2)]
        it = [sb(f"it{n}", [P, 2, MB, P], F16) for n in range(2)]
        y = [sb(f"y{n}", [P, C], F32) for n in range(2)]
        ps_x = banks(nc, held, ["f_px0", "f_px1"], F16)
        ps_h = banks(nc, held, ["f_ph0", "f_ph1"])
        ps_i = banks(nc, held, ["f_pi0", "f_pi1"], F16)
        ps_y = banks(nc, held, ["f_py0", "f_py1"])
        with nc.Fori(0, TILES // RUN) as i, phase(nc) as (block, sem):
            x_in = [sem(f"f_x_in{n}") for n in range(3)]
            y_out = [sem(f"f_y_out{n}") for n in range(2)]
            x_turned, x_copied, hidden, gated, multiplied, high, split, i_turned, i_copied, produced, y_ready = (
                sem("f_" + n) for n in ("x_turned", "x_copied", "hidden", "gated", "multiplied", "high", "split",
                                        "i_turned", "i_copied", "produced", "y_ready"))

            @block.sync
            def _(sp):
                def store(n):
                    sp.wait_ge(y_ready, n + 1)
                    sp.dma_start(t["ys"][bass.ds(i * (RUN * P) + n * P, P), :], y[n % 2][:, :]).then_inc(y_out[n % 2], 16)

                for n in range(RUN + 3):
                    if n < RUN:
                        if n >= 3:
                            sp.wait_ge(x_turned, n - 2)
                        sp.dma_start(xs[n % 3][:, :], t["xs"][bass.ds(i * (RUN * P) + n * P, P), :]).then_inc(x_in[n % 3], 16)
                    if n % 2 == 1 and n // 2 < BACK:
                        sp.dma_start(t["res"][:, bass.ds(i * BACK + n // 2, 1), :].rearrange("p a c -> p (a c)"),
                                     t["x2"][bass.ds(i * (BACK * P) + n // 2 * P, P), :]).then_inc(t["res_in"], 16)
                    if n >= 3:
                        store(n - 3)
                for n in range(2):
                    sp.wait_ge(y_out[n], 16 * (RUN // 2))

            @block.tensor
            def _(pe):
                def turn_x(n):
                    pe.wait_ge(x_in[n % 3], 16 * (n // 3 + 1))
                    if n >= 2:
                        pe.wait_ge(x_copied, n - 1)
                    for b in range(2 * CC):
                        last = pe.transpose(ps_x[n % 2][:, b * P:(b + 1) * P], xs[n % 3][:, b * P:(b + 1) * P],
                                            k["id16"][:, :])
                    last.then_inc(x_turned, 1)

                def hide(n, e):
                    pe.wait_ge(x_copied, n + 1)
                    if n >= 2:
                        pe.wait_ge(multiplied, n - 1)
                    for m in range(TERMS * CC):
                        c, term = m // TERMS, m % TERMS
                        x_part, w_part = (0, 1, 0)[term], (0, 0, 1)[term]
                        last = pe.matmul(ps_h[n % 2][:, :], xt[n % 2][:, x_part, c, :],
                                         t["wi"][:, bass.ds(e, 1), w_part, c, :].rearrange("p a f -> p (a f)"),
                                         start=(m == 0), stop=(m == TERMS * CC - 1))
                    last.then_inc(hidden, 1)

                def turn_inner(n):
                    pe.wait_ge(split, n + 1)
                    if n >= 2:
                        pe.wait_ge(i_copied, n - 1)
                    for part in range(2):
                        for m in range(MB):
                            at = (part * MB + m) * P
                            last = pe.transpose(ps_i[n % 2][:, at:at + P], parts[n % 2][:, part, m * P:(m + 1) * P],
                                                k["id16"][:, :])
                    last.then_inc(i_turned, 1)

                def produce(n, e):
                    pe.wait_ge(i_copied, n + 1)
                    if n >= 2:
                        pe.wait_ge(y_ready, n - 1)
                    for m in range(TERMS * MB):
                        c, term = m // TERMS, m % TERMS
                        i_part, w_part = (0, 1, 0)[term], (0, 0, 1)[term]
                        last = pe.matmul(ps_y[n % 2][:, :], it[n % 2][:, i_part, c, :],
                                         t["wo"][:, bass.ds(e, 1), w_part, c, :].rearrange("p a f -> p (a f)"),
                                         start=(m == 0), stop=(m == TERMS * MB - 1))
                    last.then_inc(produced, 1)

                experts = {}
                turn_x(0)
                for n in range(RUN + 1):
                    if n < RUN:
                        experts[n] = pe.value_load(t["expert_of"][0:1, bass.ds(i * RUN + n, 1)], min_val=0, max_val=E - 1)
                        if n + 1 < RUN:
                            turn_x(n + 1)
                        hide(n, experts[n])
                    if n >= 1:
                        turn_inner(n - 1)
                        produce(n - 1, experts[n - 1])

            @block.scalar
            def _(act):
                def finish(n):
                    act.wait_ge(produced, n + 1)
                    if n >= 2:
                        act.wait_ge(y_out[n % 2], 16 * (n // 2))
                    act.copy(y[n % 2][:, :], ps_y[n % 2][:, :]).then_inc(y_ready, 1)

                for n in range(RUN):
                    act.wait_ge(hidden, n + 1)
                    act.activation(gate[n % 2][:, :], ps_h[n % 2][:, 0:FF], ACT.Silu, scale=1.0 / WSCALE).then_inc(gated, 1)
                    act.wait_ge(multiplied, n + 1)
                    act.copy(parts[n % 2][:, 0, :], inner[n % 2][:, :]).then_inc(high, 1)
                    if n >= 1:
                        finish(n - 1)
                finish(RUN - 1)

            @block.vector
            def _(dve):
                def copy_x(n):
                    dve.wait_ge(x_turned, n + 1)
                    if n >= 2:
                        dve.wait_ge(hidden, n - 1)
                    dve.tensor_copy(xt[n % 2][:, :, :, :].rearrange("p s c n -> p (s c n)"), ps_x[n % 2][:, :]).then_inc(x_copied, 1)

                copy_x(0)
                for n in range(RUN):
                    if n + 1 < RUN:
                        copy_x(n + 1)
                    dve.wait_ge(gated, n + 1)
                    dve.scalar_tensor_tensor(out=inner[n % 2][:, :], in0=ps_h[n % 2][:, FF:2 * FF],
                                             scalar=1.0 / WSCALE, in1=gate[n % 2][:, :], op0=ALU.mult,
                                             op1=ALU.mult).then_inc(multiplied, 1)
                    dve.wait_ge(high, n + 1)
                    dve.tensor_tensor(parts[n % 2][:, 1, :], inner[n % 2][:, :], parts[n % 2][:, 0, :],
                                      ALU.subtract).then_inc(split, 1)
                    dve.wait_ge(i_turned, n + 1)
                    if n >= 2:
                        dve.wait_ge(produced, n - 1)
                    dve.tensor_copy(it[n % 2][:, :, :, :].rearrange("p s m n -> p (s m n)"),
                                    ps_i[n % 2][:, 0:2 * MB * P]).then_inc(i_copied, 1)


def combine(nc, t):
    with ExitStack() as held, phase(nc) as (block, sem):
        NB = 4
        rows = [sbuf(nc, held, f"c_rows{n}", [P, TOPK, C], F32) for n in range(NB)]
        res = t["res"]
        y_in = [sem(f"c_y_in{n}") for n in range(NB)]
        out = sem("c_out")
        first, second = sem("c_first"), sem("c_second")

        @block.gpsimd
        def _(pool):
            for n in range(TT):
                if n >= NB:
                    pool.wait_ge(second, n - NB + 1)
                for c in range(TOPK):
                    pool.indirect_dma_start(
                        out=rows[n % NB][:, c, :], out_offset=None, in_=t["ys"][:, :],
                        in_offset=bass.IndirectOffsetOnAxis(ap=t["rows"][:, c, n:n + 1], axis=0)).then_inc(y_in[n % NB], 16)

        @block.vector
        def _(dve):
            for n in range(TT):
                if n == 0:
                    dve.wait_ge(t["res_in"], 16 * TT)
                dve.wait_ge(y_in[n % NB], 16 * TOPK * (n // NB + 1))
                dve.scalar_tensor_tensor(out=res[:, n, :], in0=rows[n % NB][:, 0, :],
                                         scalar=t["weights"][:, 0, n:n + 1], in1=res[:, n, :],
                                         op0=ALU.mult, op1=ALU.add).then_inc(first, 1)
                dve.wait_ge(first, n + 1)
                dve.scalar_tensor_tensor(out=res[:, n, :], in0=rows[n % NB][:, 1, :],
                                         scalar=t["weights"][:, 1, n:n + 1], in1=res[:, n, :],
                                         op0=ALU.mult, op1=ALU.add).then_inc(second, 1)

        @block.scalar
        def _(act):
            for n in range(TT):
                act.wait_ge(second, n + 1)
                act.dma_start(t["out"][n * P:(n + 1) * P, :], res[:, n, :]).then_inc(out, 16)
            act.wait_ge(out, 16 * TT)


def program(nc, x, ctx_t, wq, bq, wkv_t, bkv, wp, bp, w_gate, wi_0, wi_1, w_out, out):
    x = x.rearrange("b n c -> (b n) c")
    out = out.rearrange("b n c -> (b n) c")
    t = {"x": x, "out": out, "ctx_t": ctx_t, "wkv_t": wkv_t, "bkv": bkv, "wi_0": wi_0, "wi_1": wi_1, "w_out": w_out}
    for name, shape, dt in (
        ("q_nat", (B * N, C), F32),
        ("q_t", (2, NBLK, P, B * N), F16),
        ("o", (B * N, C), F32),
        ("x2", (B * N, C), F32),
        ("xs", (TILES * P, 2 * C), F16),
        ("ys", (TILES * P, C), F32),
    ):
        t[name] = nc.dram_tensor("d_" + name, shape, dt).ap()
    with ExitStack() as held:
        sb = lambda name, shape, dt=F32: sbuf(nc, held, name, shape, dt)
        k = make_constants(nc, held)
        k["eps"] = sb("eps", [P, 1])
        t["bk"], t["bv_row"] = sb("bk", [P, NBLK]), sb("bv_row", [P, C])
        t["fine"], t["finite"], t["unfit"] = sb("fine", [P, HB, QT]), sb("finite", [P, 1]), sb("unfit", [1, 1], I32)
        t["zero"] = sb("zero", [P, C], F16)
        t["zeroed"] = held.enter_context(nc.semaphore("zeroed"))
        with ExitStack() as early:
            t["wkv"] = sbuf(nc, early, "wkv", [P, 2, CC, 2 * C], F16)
            with ExitStack() as first:
                wq_t = sbuf(nc, first, "wq_t", [P, CC, C], BF16)
                sq_row = sbuf(nc, first, "sq_row", [P, C], F32)
                bq_row = sbuf(nc, first, "bq_row", [P, C], F32)
                with phase(nc) as (block, sem):
                    rows_in = sem("rows_in")

                    @block.sync
                    def _(sp):
                        sp.dma_start(bq_row[:, :], bq[None, :].to_broadcast([P, C])).then_inc(rows_in, 16)
                        sp.dma_start(t["bv_row"][:, :], bkv[C:2 * C][None, :].to_broadcast([P, C])).then_inc(rows_in, 16)
                        with nc.allow_non_contiguous_dma(reason="one bias for each partition"):
                            sp.dma_start(t["bk"][:, :], bkv[0:C].rearrange("(k p) -> p k", p=P)).then_inc(rows_in, 16)
                        sp.wait_ge(rows_in, 48)

                    @block.vector
                    def _(dve):
                        dve.memset(k["eps"][:, :], EPS)
                        dve.memset(t["zero"][:, :], 0.0)
                        dve.wait_ge(rows_in, 48)
                        dve.tensor_scalar(t["bk"][:, :], t["bk"][:, :], WSCALE, None, ALU.mult)

                quantize_weight(nc, k, "wq_", wq, wq_t, sq_row)
                split_kv_weight(nc, wkv_t, t["wkv"])
                project_queries(nc, k, x, wq_t, sq_row, bq_row, t["q_nat"], t["q_t"])
            attention(nc, t)
        judge_range(nc, k, t)
        unfit = nc.values_load(t["unfit"][0:1, 0:1], min_val=0, max_val=1)
        with nc.If(unfit > 0):
            attention_with_maximum(nc, k, t)

        t["bp_row"], t["sp_row"], t["wp_t"] = sb("bp_row", [P, C]), sb("sp_row", [P, C]), sb("wp_t", [P, CC, C], BF16)
        t["gate"], t["logits"] = sb("gate", [P, CC, 2 * E], F16), sb("logits", [P, TT, E])
        t["rows"], t["weights"] = sb("rows", [P, TOPK, TT], U32), sb("weights", [P, TOPK, TT])
        t["expert_of"] = sb("expert_of", [1, TILES], I32)
        gate_raw = sb("gate_raw", [P, CC, E])
        with phase(nc) as (block, sem):
            late_in, high = sem("late_in"), sem("gate_high")

            @block.sync
            def _(sp):
                sp.dma_start(t["bp_row"][:, :], bp[None, :].to_broadcast([P, C])).then_inc(late_in, 16)
                sp.dma_start(gate_raw[:, :, :], w_gate.rearrange("(c p) e -> p c e", p=P)).then_inc(late_in, 16)
                sp.wait_ge(late_in, 32)

            @block.vector
            def _(dve):
                dve.wait_ge(late_in, 32)
                dve.tensor_scalar(t["gate"][:, :, 0:E], gate_raw[:, :, :], WSCALE, None, ALU.mult).then_inc(high, 1)
                dve.wait_ge(high, 1)
                dve.scalar_tensor_tensor(out=t["gate"][:, :, E:2 * E], in0=gate_raw[:, :, :], scalar=WSCALE,
                                         in1=t["gate"][:, :, 0:E], op0=ALU.mult, op1=ALU.subtract)

        quantize_weight(nc, k, "wp_", wp, t["wp_t"], t["sp_row"])
        t["xn"] = sb("xn", [P, TT, 2 * C], F16)
        project_outputs(nc, k, t)
        t["wi"] = sb("wi_parts", [P, E, 2, CC, 2 * FF], F16)
        t["wo"] = sb("wo_parts", [P, E, 2, MB, C], F16)
        route(nc, k, t)
        t["res"] = t["xn"][:, :, :].bitcast(F32)
        t["res_in"] = held.enter_context(nc.semaphore("res_in"))
        run_experts(nc, k, t)
        combine(nc, t)


def kernel(**inputs):
    import numpy as _np
    import concourse.bacc as _bacc
    from concourse import mybir as _mybir
    from concourse.bass_utils import run_bass_kernel_spmd as _run

    nc = _bacc.Bacc("TRN2", target_bir_lowering=False, num_devices=1)
    order = [("x", (0, 1, 2)), ("ctx_2048", (0, 2, 1)), ("L0_xattn_wq", (0, 1)), ("L0_xattn_bq", (0,)),
             ("L0_xattn_wkv", (1, 0)), ("L0_xattn_bkv", (0,)), ("L0_xattn_wp", (0, 1)), ("L0_xattn_bp", (0,)),
             ("L0_ffn_w_gate", (0, 1)), ("L0_ffn_wi_0", (0, 1, 2)), ("L0_ffn_wi_1", (0, 1, 2)),
             ("L0_ffn_wo", (0, 1, 2))]
    arrays, args = {}, []
    for name, axes in order:
        a = _np.ascontiguousarray(_np.transpose(_np.asarray(inputs[name]), axes))
        arrays[f"in_{name}_dram"] = a
        args.append(nc.dram_tensor(f"in_{name}_dram", a.shape, _mybir.dt.from_np(a.dtype), kind="ExternalInput").ap())
    args.append(nc.dram_tensor("out_0_dram", (B, N, C), F32, kind="ExternalOutput").ap())
    program(nc, *args)
    r = _run(nc, [arrays], core_ids=[0])
    return r.results[0]["out_0_dram"]
```
